# Optimizing a Trainium2 kernel written in Bass

```python
import numpy as np
import jax
import jax.numpy as jnp

def _softmax(x, axis=-1):
    return jax.nn.softmax(x, axis=axis)

def _gelu(x):
    return jax.nn.gelu(x, approximate=True)

def _silu(x):
    return jax.nn.silu(x)

def _sigmoid(x):
    return jax.nn.sigmoid(x)

def _layernorm(x, axis=-1, eps=1e-05):
    m = jnp.mean(x, axis=axis, keepdims=True)
    v = jnp.var(x, axis=axis, keepdims=True)
    return (x - m) / jnp.sqrt(v + eps)

def _scatter_add(tgt, idx, src, axis=0):
    return tgt.at[idx].add(src)

def _segment_sum(src, seg, n):
    return jax.ops.segment_sum(src, seg, n)
kernel_name = 'mk_decoder_preln_d1_seqx_r4_7ab21e'

def setup_inputs(seed: int=0):
    np.random.seed(seed)
    _w = jnp.asarray

    def _rec_inputs():
        import jax
        import jax.numpy as jnp
        _rk = jax.random.key(seed)
        x = 7.22e-05 + 1 * jax.random.normal(jax.random.fold_in(_rk, 1), (16, 100, 512), jnp.float32)
        _lenS = 100 - jax.random.randint(jax.random.fold_in(_rk, 7), (16,), 0, max(1, 100 // 4) + 1, jnp.int32)
        _lenS2 = 361 - jax.random.randint(jax.random.fold_in(_rk, 8), (16,), 0, max(1, 361 // 4) + 1, jnp.int32)
        _ctx_512P = jax.random.normal(jax.random.fold_in(_rk, 11), (16, 16, 128), jnp.float32)
        _ctx_512c = jax.random.dirichlet(jax.random.fold_in(_rk, 511), 0.3 * jnp.ones((16,), jnp.float32), (16, 361))
        _ctx_512t = jnp.einsum('bsk,bkd->bsd', _ctx_512c, _ctx_512P)
        _ctx_512t = _ctx_512t * jax.lax.rsqrt(jnp.mean(jnp.square(_ctx_512t)) + 1e-12) * 0.953939
        ctx_512 = -0.000514642 + 1.00011 * (_ctx_512t + 0.3 * jax.random.normal(jax.random.fold_in(_rk, 611), (16, 361, 128), jnp.float32))
        return (x, ctx_512)
    x, ctx_512 = _rec_inputs()

    def _L0_attn_setup():
        import jax, jax.numpy as jnp
        import numpy as np
        B, T, HID = (2, 512, 512)
        H, D, QC = (16, 128, 128)
        RD, THETA = (64, 10000.0)
        WIN = 128
        G, INTER = (4, 512)
        EPS = 1e-06

        def _rope_cache(t):
            inv = 1.0 / THETA ** (jnp.arange(0, RD, 2, dtype=jnp.float32) / RD)
            ang = jnp.arange(t, dtype=jnp.float32)[:, None] * inv[None, :]
            return (jnp.cos(ang), jnp.sin(ang))

        def _apply_partial_rope(x, cos, sin):
            x_rot, x_pass = (x[..., :RD], x[..., RD:])
            x1, x2 = (x_rot[..., :RD // 2], x_rot[..., RD // 2:])
            r1 = x1 * cos - x2 * sin
            r2 = x1 * sin + x2 * cos
            return jnp.concatenate([r1, r2, x_pass], axis=-1)

        def _rmsnorm(x, w):
            return x * jax.lax.rsqrt(jnp.mean(x * x, axis=-1, keepdims=True) + EPS) * w
        key = jax.random.key(seed)
        ks = jax.random.split(key, 10)
        s = 0.02
        return {'h': jax.random.normal(ks[0], (B, T, HID), jnp.float32), 'wq_comp': jax.random.normal(ks[1], (HID, QC), jnp.float32) * s, 'wq_up': jax.random.normal(ks[2], (QC, H * D), jnp.float32) * s, 'wk': jax.random.normal(ks[3], (HID, D), jnp.float32) * s, 'wv': jax.random.normal(ks[4], (HID, D), jnp.float32) * s, 'q_norm_w': jnp.ones((D,), jnp.float32), 'k_norm_w': jnp.ones((D,), jnp.float32), 'sink_logit': jnp.zeros((H,), jnp.float32), 'out_w1': jax.random.normal(ks[5], (G, H // G * D, INTER), jnp.float32) * s, 'out_w2': jax.random.normal(ks[6], (G * INTER, HID), jnp.float32) * s}
    _L0_attn_all = _L0_attn_setup()
    _L0_attn_in = {k: v for k, v in _L0_attn_all.items() if k in ('wq_comp', 'wq_up', 'wk', 'wv', 'q_norm_w', 'k_norm_w', 'sink_logit', 'out_w1', 'out_w2')}
    del _L0_attn_all

    def _L0_xattn_setup():
        import jax, jax.numpy as jnp
        import numpy as np
        B, S, H, NH, L = (2, 512, 512, 16, 128)
        HD = H // NH
        key = jax.random.key(seed)
        k1, k2, k3, k4, k5 = jax.random.split(key, 5)
        scale = 0.02
        return {'q': jax.random.normal(k1, (B, S, H), dtype=jnp.float32), 'latent_kv': jax.random.normal(k2, (B, S, L), dtype=jnp.float32), 'Wq': jax.random.normal(k3, (H, H), dtype=jnp.float32) * scale, 'Wkv_expand': jax.random.normal(k4, (2 * H, L), dtype=jnp.float32) * scale, 'Wout': jax.random.normal(k5, (H, H), dtype=jnp.float32) * scale}
    _L0_xattn_all = _L0_xattn_setup()
    _L0_xattn_in = {k: v for k, v in _L0_xattn_all.items() if k in ('Wq', 'Wkv_expand', 'Wout')}
    del _L0_xattn_all

    def _L0_ffn_setup():
        import jax, jax.numpy as jnp
        import numpy as np
        from jax import lax
        H = 512
        I = 256
        E = 32
        K = 4
        SH_I = 512
        EPS = 1e-06

        def _rmsnorm(x, w, eps=EPS):
            var = jnp.mean(jnp.square(x.astype(jnp.float32)), axis=-1, keepdims=True)
            return (x * lax.rsqrt(var + eps)).astype(x.dtype) * w
        key = jax.random.key(seed)
        ks = jax.random.split(key, 8)
        s = lambda d: 1.0 / np.sqrt(d)
        return {'x': jax.random.normal(ks[0], (2, 512, H), jnp.float32), 'norm_w': jnp.ones((H,), jnp.float32), 'router_w': jax.random.normal(ks[1], (E, H), jnp.float32) * s(H), 'w1': jax.random.normal(ks[2], (E, H, 2 * I), jnp.float32) * s(H), 'w2': jax.random.normal(ks[3], (E, I, H), jnp.float32) * s(I), 'sg': jax.random.normal(ks[4], (H, SH_I), jnp.float32) * s(H), 'su': jax.random.normal(ks[5], (H, SH_I), jnp.float32) * s(H), 'sd': jax.random.normal(ks[6], (SH_I, H), jnp.float32) * s(SH_I)}
    _L0_ffn_all = _L0_ffn_setup()
    _L0_ffn_in = {k: v for k, v in _L0_ffn_all.items() if k in ('norm_w', 'router_w', 'w1', 'w2', 'sg', 'su', 'sd')}
    del _L0_ffn_all
    return {'x': x, 'ctx_512': ctx_512, 'L0_attn_wq_comp': _L0_attn_in['wq_comp'], 'L0_attn_wq_up': _L0_attn_in['wq_up'], 'L0_attn_wk': _L0_attn_in['wk'], 'L0_attn_wv': _L0_attn_in['wv'], 'L0_attn_q_norm_w': _L0_attn_in['q_norm_w'], 'L0_attn_k_norm_w': _L0_attn_in['k_norm_w'], 'L0_attn_sink_logit': _L0_attn_in['sink_logit'], 'L0_attn_out_w1': _L0_attn_in['out_w1'], 'L0_attn_out_w2': _L0_attn_in['out_w2'], 'L0_xattn_Wq': _L0_xattn_in['Wq'], 'L0_xattn_Wkv_expand': _L0_xattn_in['Wkv_expand'], 'L0_xattn_Wout': _L0_xattn_in['Wout'], 'L0_ffn_norm_w': _L0_ffn_in['norm_w'], 'L0_ffn_router_w': _L0_ffn_in['router_w'], 'L0_ffn_w1': _L0_ffn_in['w1'], 'L0_ffn_w2': _L0_ffn_in['w2'], 'L0_ffn_sg': _L0_ffn_in['sg'], 'L0_ffn_su': _L0_ffn_in['su'], 'L0_ffn_sd': _L0_ffn_in['sd']}

def reference(x, ctx_512, L0_attn_wq_comp, L0_attn_wq_up, L0_attn_wk, L0_attn_wv, L0_attn_q_norm_w, L0_attn_k_norm_w, L0_attn_sink_logit, L0_attn_out_w1, L0_attn_out_w2, L0_xattn_Wq, L0_xattn_Wkv_expand, L0_xattn_Wout, L0_ffn_norm_w, L0_ffn_router_w, L0_ffn_w1, L0_ffn_w2, L0_ffn_sg, L0_ffn_su, L0_ffn_sd):
    import jax
    import jax.numpy as jnp

    def _L0_attn_ref(h, wq_comp, wq_up, wk, wv, q_norm_w, k_norm_w, sink_logit, out_w1, out_w2):
        import jax, jax.numpy as jnp
        import numpy as np
        B, T, HID = (2, 512, 512)
        H, D, QC = (16, 128, 128)
        RD, THETA = (64, 10000.0)
        WIN = 128
        G, INTER = (4, 512)
        EPS = 1e-06

        def _rope_cache(t):
            inv = 1.0 / THETA ** (jnp.arange(0, RD, 2, dtype=jnp.float32) / RD)
            ang = jnp.arange(t, dtype=jnp.float32)[:, None] * inv[None, :]
            return (jnp.cos(ang), jnp.sin(ang))

        def _apply_partial_rope(x, cos, sin):
            x_rot, x_pass = (x[..., :RD], x[..., RD:])
            x1, x2 = (x_rot[..., :RD // 2], x_rot[..., RD // 2:])
            r1 = x1 * cos - x2 * sin
            r2 = x1 * sin + x2 * cos
            return jnp.concatenate([r1, r2, x_pass], axis=-1)

        def _rmsnorm(x, w):
            return x * jax.lax.rsqrt(jnp.mean(x * x, axis=-1, keepdims=True) + EPS) * w
        b, t, _ = h.shape
        cos, sin = _rope_cache(t)
        q = h @ wq_comp @ wq_up
        q = q.reshape(b, t, H, D).transpose(0, 2, 1, 3)
        q = _rmsnorm(_apply_partial_rope(q, cos, sin), q_norm_w)
        k = _rmsnorm(_apply_partial_rope(h @ wk, cos, sin), k_norm_w)
        v = h @ wv
        i = jnp.arange(t)
        diff = i[:, None] - i[None, :]
        mask = (diff >= 0) & (diff < WIN)
        scale = 1.0 / jnp.sqrt(jnp.asarray(D, h.dtype))
        scores = jnp.einsum('bhtd,bsd->bhts', q, k) * scale
        scores = jnp.where(mask[None, None], scores, jnp.asarray(-1e+30, h.dtype))
        sink = jnp.broadcast_to(sink_logit[None, :, None, None], (b, H, t, 1))
        probs = jax.nn.softmax(jnp.concatenate([scores, sink], axis=-1), axis=-1)
        attn = jnp.einsum('bhts,bsd->bhtd', probs[..., :t], v)
        x = attn.transpose(0, 2, 1, 3).reshape(b, t, G, H // G * D)
        x = jnp.einsum('btgi,gio->btgo', x, out_w1).reshape(b, t, G * INTER)
        return x @ out_w2

    def _L0_xattn_ref(q, latent_kv, Wq, Wkv_expand, Wout):
        import jax, jax.numpy as jnp
        import numpy as np
        B, S, H, NH, L = (2, 512, 512, 16, 128)
        HD = H // NH
        b, sq, _ = q.shape
        sk = latent_kv.shape[1]
        qp = q @ Wq.T
        kv = latent_kv @ Wkv_expand.T
        k, v = jnp.split(kv, 2, axis=-1)
        qh = qp.reshape(b, sq, NH, HD).transpose(0, 2, 1, 3)
        kh = k.reshape(b, sk, NH, HD).transpose(0, 2, 1, 3)
        vh = v.reshape(b, sk, NH, HD).transpose(0, 2, 1, 3)
        inv_sqrt_d = 1.0 / jnp.sqrt(jnp.float32(HD))
        scores = jnp.einsum('bhqd,bhkd->bhqk', qh, kh) * inv_sqrt_d
        causal = jnp.tril(jnp.ones((sq, sk), dtype=bool))
        scores = jnp.where(causal, scores, jnp.finfo(scores.dtype).min)
        attn = jax.nn.softmax(scores, axis=-1)
        out = jnp.einsum('bhqk,bhkd->bhqd', attn, vh)
        out = out.transpose(0, 2, 1, 3).reshape(b, sq, H)
        return out @ Wout.T

    def _L0_ffn_ref(x, norm_w, router_w, w1, w2, sg, su, sd):
        import jax, jax.numpy as jnp
        import numpy as np
        from jax import lax
        H = 512
        I = 256
        E = 32
        K = 4
        SH_I = 512
        EPS = 1e-06

        def _rmsnorm(x, w, eps=EPS):
            var = jnp.mean(jnp.square(x.astype(jnp.float32)), axis=-1, keepdims=True)
            return (x * lax.rsqrt(var + eps)).astype(x.dtype) * w
        B, S, _ = x.shape
        residual = x
        h = _rmsnorm(x, norm_w)
        flat = h.reshape(-1, H)
        T = flat.shape[0]
        logits = flat.astype(jnp.float32) @ router_w.T
        scores = jax.nn.softmax(logits, axis=-1)
        topk_w, topk_ids = lax.top_k(scores, K)
        topk_w = topk_w / jnp.sum(topk_w, axis=-1, keepdims=True)
        ids = topk_ids.reshape(-1)
        sort_idx = jnp.argsort(ids)
        tok_idx = sort_idx // K
        xs = jnp.take(flat, tok_idx, axis=0)
        group_sizes = jnp.bincount(ids, length=E).astype(jnp.int32)
        gu = lax.ragged_dot(xs, w1, group_sizes)
        g, u = jnp.split(gu, 2, axis=-1)
        act = jax.nn.silu(g) * u
        ys = lax.ragged_dot(act, w2, group_sizes)
        y = jnp.zeros((T * K, H), ys.dtype).at[sort_idx].set(ys)
        routed = jnp.sum(y.reshape(T, K, H) * topk_w[..., None].astype(ys.dtype), axis=1)
        shared = jax.nn.silu(flat @ sg) * (flat @ su) @ sd
        out = residual + (routed + shared).reshape(B, S, H)
        return out
    x = x + _L0_attn_ref(_layernorm(x, axis=-1), L0_attn_wq_comp, L0_attn_wq_up, L0_attn_wk, L0_attn_wv, L0_attn_q_norm_w, L0_attn_k_norm_w, L0_attn_sink_logit, L0_attn_out_w1, L0_attn_out_w2)
    x = x + _L0_xattn_ref(_layernorm(x, axis=-1), ctx_512, L0_xattn_Wq, L0_xattn_Wkv_expand, L0_xattn_Wout)
    x = x + _L0_ffn_ref(_layernorm(x, axis=-1), L0_ffn_norm_w, L0_ffn_router_w, L0_ffn_w1, L0_ffn_w2, L0_ffn_sg, L0_ffn_su, L0_ffn_sd)
    return x

_drawn_inputs = setup_inputs


def setup_inputs(seed=0):
    import zlib

    import numpy as np

    out = dict(_drawn_inputs(seed))
    spreads = {'L0_attn_q_norm_w': (1.0, 0.6),
     'L0_attn_k_norm_w': (1.0, 0.6),
     'L0_attn_sink_logit': (0.0, 0.8),
     'L0_ffn_norm_w': (1.0, 0.2)}
    factors = {'L0_xattn_Wq': 8.0}
    for name, (base, spread) in spreads.items():
        noise = np.random.default_rng([zlib.crc32(name.encode()), seed]).standard_normal(out[name].shape)
        drawn = base * np.exp(spread * noise) if base else spread * noise
        out[name] = jnp.asarray(drawn.astype(out[name].dtype))
    for name, factor in factors.items():
        out[name] = (out[name] * factor).astype(out[name].dtype)
    return out
```

```python
import math
from contextlib import ExitStack

import concourse.bass as bass
from concourse import mybir

NB, T, HID = 16, 100, 512
NH, D = 16, 128
RD = 64
NX, DX = 16, 32
G, GI = 4, 512
NE, TOPK, FE = 32, 4, 256
FS = 512
P = 128
KC = HID // P
NTOK = NB * T
QH = 4
QW = QH * T
BLK = 128
FAST = 2
NBLK = -(-NTOK // BLK)
CAP = NBLK * BLK
PADS = FAST * BLK
ROWS = NTOK + PADS
HXW = HID + NE
RING = 4
WX = KC * 2 * FE + (FE // P) * HID
NEG = -1e30

fp32, bf16 = mybir.dt.float32, mybir.dt.bfloat16
i32, u32 = mybir.dt.int32, mybir.dt.uint32
ALU, ACT, AX = mybir.AluOpType, mybir.ActivationFunctionType, mybir.AxisListType

class Signals:
    def __init__(self, new):
        self.ld_x0, self.ld_x, self.ld_const, self.ld_w, self.ld_wx, self.ld_half0 = new("ld_x0 ld_x ld_const ld_w ld_wx ld_half0")
        self.ld_half1, self.ld_ctx, self.ld_sh, self.wqk, self.passed = new("ld_half1 ld_ctx ld_sh wqk passed")
        self.wc_ps, self.wc = new("wc_ps wc")
        self.ln1_stats, self.ln1_mv, self.ln1_var, self.ln1_rstd, self.ln1_h, self.ln2_stats = new("ln1_stats ln1_mv ln1_var ln1_rstd ln1_h ln2_stats")
        self.ln2_mv, self.ln2_var, self.ln2_rstd, self.ln2_h = new("ln2_mv ln2_var ln2_rstd ln2_h")
        self.ln3_stats, self.ln3_mv, self.ln3_var, self.ln3_rstd, self.ln3_xc, self.ln3_g = new("ln3_stats ln3_mv ln3_var ln3_rstd ln3_xc ln3_g")
        self.ln3_h, self.ln3_base = new("ln3_h ln3_base")
        self.h1T_ps, self.h1T, self.hq_ps, self.hqT, self.kv_ps, self.kv = new("h1T_ps h1T hq_ps hqT kv_ps kv")
        self.v, self.q_ps, self.q_out, self.q_parts, self.q_rot, self.q_ssq = new("v q_ps q_out q_parts q_rot q_ssq")
        self.qk_var, self.qk_rstd = new("qk_var qk_rstd")
        self.k_parts, self.k_rot, self.k_scaled, self.kT_ps, self.kT, self.qT_ps = new("k_parts k_rot k_scaled kT_ps kT qT_ps")
        self.qT = new("qT")[0]
        self.s_ps, self.s_scaled, self.s_max, self.s_top, self.s_shift, self.s_sink = new("s_ps s_scaled s_max s_top s_shift s_sink")
        self.p_exp, self.e_sink, self.p_sum, self.p_den, self.p_inv, self.p_norm = new("p_exp e_sink p_sum p_den p_inv p_norm")
        self.pT_ps, self.pT, self.o_ps, self.oT, self.x1_ps, self.x1 = new("pT_ps pT o_ps oT x1_ps x1")
        self.h2T_ps, self.h2T, self.ck_ps, self.ck, self.cv_ps, self.cv = new("h2T_ps h2T ck_ps ck cv_ps cv")
        self.qp_ps, self.qp, self.sx_ps, self.sx, self.sx_max, self.sx_shift = new("qp_ps qp sx_ps sx sx_max sx_shift")
        self.px_exp, self.px_sum, self.px_inv, self.pxT_ps, self.pxT, self.avx_ps = new("px_exp px_sum px_inv pxT_ps pxT avx_ps")
        self.ox, self.oxT_ps, self.oxT, self.x2_ps, self.x2 = new("ox oxT_ps oxT x2_ps x2")
        self.h3T_ps, self.h3s, self.h3T, self.lg_ps, self.lg, self.top8 = new("h3T_ps h3s h3T lg_ps lg top8")
        self.topi, self.topd, self.top_exp, self.top_inv, self.top_w, self.onehot = new("topi topd top_exp top_inv top_w onehot")
        self.chosen, self.ohw, self.wd, self.hx_st = new("chosen ohw wd hx_st")
        self.rank_ps, self.rank, self.rank_used, self.picked, self.slots, self.scat = new("rank_ps rank rank_used picked slots scat")
        self.sh_g, self.sh_u, self.sh_silu, self.sh_act, self.sh_y_ps, self.sh_y = new("sh_g sh_u sh_silu sh_act sh_y_ps sh_y")
        self.sh_st0, self.sh_st1, self.pad_st = new("sh_st0 sh_st1 pad_st")
        self.ix_ld, self.ix_f, self.ix_T, self.idx, self.cnt_f, self.cnt = new("ix_ld ix_f ix_T idx cnt_f cnt")


class ExpertSignals:
    def __init__(self, new):
        self.xT_ps, self.xT, self.gu_ps, self.act_s, self.act = new("xT_ps xT gu_ps act_s act")
        self.y_ps, self.y_w, self.scat_add, self.ix, self.wcol = new("y_ps y_w scat_add ix wcol")


class LateSignals:
    def __init__(self, new):
        self.w, self.idx, self.g, self.xT_ps, self.xT, self.gu_ps = new("w idx g xT_ps xT gu_ps")
        self.act_s, self.act, self.y_ps, self.y_w, self.add = new("act_s act y_ps y_w add")


class Stages:
    def __init__(self, A, Q, X, C):
        self.A, self.Q, self.X, self.C = A, Q, X, C


def build(nc, a, out):
    with ExitStack() as ctx:
        def sb(name, shape, dt=fp32):
            return ctx.enter_context(nc.sbuf_tensor(name, shape, dt))

        def semaphores(prefix):
            return lambda names: [ctx.enter_context(nc.semaphore(prefix + n)) for n in names.split()]

        s, m, o = Signals(semaphores("")), ExpertSignals(semaphores("m_")), LateSignals(semaphores("o_"))
        s.ring = [ctx.enter_context(nc.semaphore(f"ring{i}")) for i in range(RING)]
        s.gath = [ctx.enter_context(nc.semaphore(f"gath{i}")) for i in range(2)]

        w_all = sb("w_all", [P, 32 * 256 + 34 * 256])
        wc = w_all[:, 0:8192]
        w_up = w_all[:, 8192:10240]
        w_kv = w_all[:, 10240:11264]
        w_q = w_all[:, 11264:13312]
        w_kx = w_all[:, 13312:14336]
        w_out = w_all[:, 14336:16384]
        w_comp = w_all[:, 16384:16896]
        w_sg, w_su, w_sd = (w_all[:, 2048 * i:2048 * (i + 1)] for i in range(3))
        w_r = sb("w_r", [P, KC * NE])

        work = sb("work", [P, 4 * 1600 + 2048 + 1024 + 3 * 512])
        T16, Pm, PX, OT = (work[:, 1600 * i:1600 * (i + 1)] for i in range(4))
        qr = work[0:T, 6400:8448]
        rtmp = work[0:T, 8448:9472]
        h1, h2, xc = (work[0:T, 9472 + 512 * i:9984 + 512 * i] for i in range(3))
        resid = sb("resid", [T, NB * HID])
        h3T = sb("h3T", [P, KC * NTOK])
        h3x = sb("h3x", [T, HXW])
        h1T, h2T, h3s, qpT, ckT, oxT = (sb(n, [P, 400]) for n in ("h1T", "h2T", "h3s", "qpT", "ckT", "oxT"))
        hqT, kT, ctxT = (sb(n, [P, T]) for n in ("hqT", "kT", "ctxT"))
        kvs, vS, kr, ktmp = sb("kvs", [T, 2 * D]), sb("vS", [T, D]), sb("kr", [T, D]), sb("ktmp", [T, RD])
        cv, ox, junk = sb("cv", [T, HID]), sb("ox", [T, HID]), sb("junk", [T, D])
        ssq, qkv_var, rall, phalf = (sb(n, [T, NH + 1]) for n in ("ssq", "qkv_var", "rall", "phalf"))
        mx, sdiff, esink, den, rinv, mxx, denx, rx = (
            sb(n, [T, NH]) for n in ("mx", "sdiff", "esink", "den", "rinv", "mxx", "denx", "rx"))
        st = [sb(f"st{k}", [T, 6]) for k in range(3)]
        mv = [sb(f"mv{k}", [T, 2]) for k in range(3)]
        var = [sb(f"var{k}", [T, 2]) for k in range(3)]
        rstd = [sb(f"rstd{k}", [T, 2]) for k in range(3)]
        lgs, v8, i8, idxf = sb("lgs", [T, NE]), sb("v8", [T, 8]), sb("i8", [T, 8], u32), sb("idxf", [T, TOPK])
        d4, e4, sum4, inv4, w4 = (sb(n, [T, k]) for n, k in (("d4", 4), ("e4", 4), ("sum4", 1), ("inv4", 1), ("w4", 4)))
        oh, ohw, pick = sb("oh", [T, TOPK * NE]), sb("ohw", [T, TOPK * NE]), sb("pick", [T, TOPK * NE])
        chosen = sb("chosen", [T, NE], bf16)
        rk, run = sb("rk", [T, NE]), sb("run", [T, NE])
        slot, tok = sb("slot", [T, TOPK], i32), sb("tok", [T, 1], i32)
        ident, c64, s64 = sb("ident", [P, P]), sb("c64", [T, RD]), sb("s64", [T, RD])
        eid, runs, tokall = sb("eid", [T, TOPK * NE]), sb("runs", [T, NE]), sb("tokall", [T, NB], i32)
        identb, mask4 = sb("identb", [T, T], bf16), sb("mask4", [T, QW], bf16)
        tri, ones = sb("tri", [T, T], bf16), sb("ones", [T, T], bf16)
        wqk, wkn, sink, normw = sb("wqk", [T, D]), sb("wkn", [T, D]), sb("sink", [T, NH]), sb("normw", [T, HID])
        shact, shtmp = sb("shact", [P, 4 * QW]), ckT
        ytile = [sb(f"ytile{i}", [T, HID]) for i in range(2)]
        slots_w = [w_all[:, 6144 + WX * i:6144 + WX * (i + 1)] for i in range(3)] + [work[:, 0:WX]]
        w1s = [w[:, 0:2048] for w in slots_w]
        w2s = [w[:, 2048:3072] for w in slots_w]
        at = WX
        Xg = [[work[:, at + (2 * i + j) * HXW:at + (2 * i + j + 1) * HXW] for j in range(2)] for i in range(2)]
        at += 4 * HXW
        XT = [work[:, at + 1024 * i:at + 1024 * (i + 1)] for i in range(2)]
        at += 2048
        ea = work[:, at:at + 512]
        at += 512
        et = work[:, at:at + 512]
        at += 512
        Y = [work[:, at + 1024 * i:at + 1024 * (i + 1)] for i in range(2)]
        ixr, ixf = h1T[0:2 * NE, 0:P].bitcast(i32), h2T[0:2 * NE, 0:P]
        idx = sb("idx", [P, 2 * NE], i32)
        ixs = [sb(f"ixs{i}", [P, FAST], i32) for i in range(RING)]
        wcol = [sb(f"wcol{i}", [P, FAST]) for i in range(RING)]
        cnt, most = sb("cnt", [1, NE], i32), sb("most", [1, 1], i32)
        oidx = kT[:, 0:1].bitcast(i32)

        QS = ctx.enter_context(nc.psum_tensor("QS", [P, 2048], fp32))
        W = ctx.enter_context(nc.psum_tensor("W", [P, 2048], fp32))
        qb = [QS[:, 512 * i:512 * (i + 1)] for i in range(4)]
        wb = [W[:, 512 * i:512 * (i + 1)] for i in range(4)]

        hx = nc.dram_tensor("hx_rows", [ROWS, HXW], fp32, kind="Internal").ap()
        table = nc.dram_tensor("expert_lists", [NE * CAP, 1], i32, kind="Internal").ap()

        half = [[h3T[:, 0:2048], h3T[:, 2048:4096]], [work[:, 0:2048], work[:, 2048:4096]]]
        block = ctx.enter_context(nc.Block())

        def wait_alone(eng, sem, value):
            eng.wait_ge(sem, value)
            eng.sem_inc(s.passed, 1)

        def stages(b):
            if isinstance(b, int):
                return Stages(A=b < NB, Q=b + 1 < NB, X=1 <= b <= NB, C=b >= 2)
            return Stages(A=True, Q=True, X=True, C=True)

        def pipeline(eng, step):
            step(0)
            step(1)
            with eng.Fori(2, NB - 1) as b:
                step(b)
            for b in range(NB - 1, NB + 2):
                step(b)

        @block.sync
        def _(sp):
            xv = a["x"].rearrange("b t d -> t b d")
            rv = resid[:, :].rearrange("t (b d) -> t b d", d=HID)
            consts = [(ident, "c_ident"), (c64, "c_cos"), (s64, "c_sin"), (eid, "c_eid"), (runs, "c_runs"),
                      (tokall, "c_tok"), (identb, "c_identb"), (mask4, "c_mask"), (tri, "c_tri"), (ones, "c_ones"),
                      (wqk, "qn"), (wkn, "kn"), (sink, "sink"), (normw, "normw")]
            for g in range(G):
                if g >= 2:
                    sp.wait_ge(s.wc_ps, 4 * (g - 1))
                h, done = half[g % 2], (s.ld_half0, s.ld_half1)[g % 2]
                sp.dma_start(h[0].rearrange("p (k n) -> p k n", k=4),
                             a["w1T"][g].rearrange("(k p) n -> p k n", p=P)).then_inc(done, 16)
                sp.dma_start(h[1].rearrange("p (k n) -> p k n", k=4),
                             a["out_w2"][GI * g:GI * (g + 1), :].rearrange("(k p) n -> p k n", p=P)).then_inc(done, 16)
                if g == 0:
                    sp.dma_start(rv[:, 0:1, :], xv[:, 0:1, :]).then_inc(s.ld_x0, 16)
                    for t, n in consts:
                        sp.dma_start(t[:, :], a[n]).then_inc(s.ld_const, 16)
                if g == 1:
                    for t, n, k in ((w_comp, "wq_comp", KC), (w_up, "wq_up", 1), (w_kv, "wkv", KC)):
                        sp.dma_start(t.rearrange("p (k n) -> p k n", k=k),
                                     a[n].rearrange("(k p) n -> p k n", p=P)).then_inc(s.ld_w, 16)
                if g == 2:
                    sp.dma_start(rv[:, 1:NB, :], xv[:, 1:NB, :]).then_inc(s.ld_x, 16)
            for t, n, k in ((w_q, "WqT", KC), (w_kx, "WkvT", 1), (w_out, "WoutT", KC), (w_r, "routerT", KC)):
                sp.dma_start(t.rearrange("p (k n) -> p k n", k=k) if n != "routerT" else
                             t[:, :].rearrange("p (k n) -> p k n", k=k),
                             a[n].rearrange("(k p) n -> p k n", p=P)).then_inc(s.ld_wx, 16)
            sp.dma_start(table, a["c_table"]).then_inc(s.pad_st, 16)
            sp.dma_start(hx[NTOK:ROWS, :], a["c_zero"]).then_inc(s.pad_st, 16)
            sp.dma_start(out[NTOK:ROWS, :], a["c_zero"][:, 0:HID]).then_inc(s.pad_st, 16)

            def step(b):
                do = stages(b)
                if do.A:
                    src = a["ctxT"][bass.ds(b, 1), :, 0:T].rearrange("b k t -> (b k) t")
                    sp.wait_ge(s.cv_ps, b)
                    sp.dma_start(ctxT[:, :], src).then_inc(s.ld_ctx, 16)
                if isinstance(b, int) and b == NB:
                    sp.wait_ge(s.x1_ps, NB)
                    for t, n in ((w_sg, "sg"), (w_su, "su"), (w_sd, "sd")):
                        sp.dma_start(t.rearrange("p (k n) -> p k n", k=KC),
                                     a[n].rearrange("(k p) n -> p k n", p=P)).then_inc(s.ld_sh, 16)
                if do.C:
                    dst = hx[bass.ds(sp.snap(T * (b - 2)) if not isinstance(b, int) else T * (b - 2), T), :]
                    sp.wait_ge(s.wd, b - 1)
                    sp.dma_start(dst, h3x[:, :]).then_inc(s.hx_st, 16)

            pipeline(sp, step)

            sp.wait_ge(s.x2_ps, NB)

            def load_expert(e, u):
                src1 = a["w1"][bass.ds(e, 1), :, :].rearrange("e (k p) n -> p (e k) n", p=P)
                src2 = a["w2"][bass.ds(e, 1), :, :].rearrange("e (k p) n -> p (e k) n", p=P)
                return ((w1s[u].rearrange("p (k n) -> p k n", k=KC), src1),
                        (w2s[u].rearrange("p (k n) -> p k n", k=FE // P), src2))

            for u in range(RING):
                for dst, src in load_expert(u, u):
                    sp.dma_start(dst, src).then_inc(s.ring[u], 16)
            with sp.Fori(1, NE // RING) as r:
                e = r * RING
                for u in range(RING):
                    pair = load_expert(e + u, u)
                    sp.wait_ge(m.y_ps, e + u - (RING - 1))
                    for dst, src in pair:
                        sp.dma_start(dst, src).then_inc(s.ring[u], 16)

            done = sp.alloc_register("sp_late")
            sp.reg_mov(done, 0)
            sp.wait_ge(s.cnt, 2)
            longest = sp.value_load(most[0:1, 0:1], min_val=0, max_val=NTOK)
            with sp.If(longest > BLK * FAST):
                with sp.Fori(0, NE) as e:
                    c = sp.value_load(cnt[0:1, bass.ds(e, 1)], min_val=0, max_val=NTOK)
                    with sp.If(c > BLK * FAST):
                        with sp.Fori(FAST, NBLK) as j:
                            with sp.If(c > BLK * j):
                                k = sp.snap(done)
                                pair = load_expert(e, 0)
                                isrc = table[bass.ds(CAP * e + BLK * j, BLK), :]
                                sp.wait_ge(m.y_ps, NE)
                                sp.wait_ge(o.add, 16 * k)
                                for dst, src in pair:
                                    sp.dma_start(dst, src).then_inc(o.w, 16)
                                sp.dma_start(oidx, isrc).then_inc(o.idx, 16)
                                sp.reg_add(done, done, 1)
                                sp.nop(nofuse=True)
                        sp.nop(nofuse=True)
                sp.nop(nofuse=True)

        @block.tensor
        def _(pe):
            mm, tr = nc.tensor.matmul, nc.tensor.transpose
            def join(g):
                pe.wait_ge((s.ld_half0, s.ld_half1)[g % 2], 32 * (g // 2 + 1))
                for i in range(4):
                    n = 4 * g + i
                    if n >= 4:
                        pe.wait_ge(s.wc, n - 3)
                    if n == 14:
                        pe.wait_ge(s.kv, 1)
                    for k in range(4):
                        w1, w2 = half[g % 2]
                        last = mm(wb[n % 4], w1[:, 512 * k + P * i:512 * k + P * (i + 1)],
                                  w2[:, 512 * k:512 * (k + 1)], start=k == 0, stop=k == 3)
                    last.then_inc(s.wc_ps, 1)

            def to_columns(dst, src, n=KC, w=P):
                for k in range(n):
                    last = tr(dst[0:w, T * k:T * (k + 1)], src[0:T, w * k:w * (k + 1)], ident[0:T, 0:T])
                return last

            def ln1_columns(c):
                pe.wait_ge(s.ln1_h, c + 1)
                to_columns(wb[0], h1).then_inc(s.h1T_ps, 1)

            def compress(c):
                pe.wait_ge(s.h1T, c + 1)
                for k in range(KC):
                    last = mm(wb[1][:, 0:T], w_comp[:, P * k:P * (k + 1)], h1T[:, T * k:T * (k + 1)],
                              start=k == 0, stop=k == KC - 1)
                last.then_inc(s.hq_ps, 1)
                for k in range(KC):
                    last = mm(wb[2][0:T, 0:2 * D], h1T[:, T * k:T * (k + 1)], w_kv[:, 256 * k:256 * (k + 1)],
                              start=k == 0, stop=k == KC - 1)
                last.then_inc(s.kv_ps, 1)

            def queries(c):
                pe.wait_ge(s.hqT, c + 1)
                for i in range(4):
                    last = mm(qb[i][0:T, :], hqT[:, :], w_up[:, 512 * i:512 * (i + 1)], start=True, stop=True)
                last.then_inc(s.q_ps, 1)

            def project(b, heads):
                for h in heads:
                    if h % QH == 0:
                        pe.wait_ge(s.oT, 4 * b + h // QH + 1)
                    last = mm(wb[0][0:T, :], OT[:, T * h:T * (h + 1)], wc[:, 512 * h:512 * (h + 1)],
                              start=h == 0, stop=h == NH - 1)
                return last

            def step(b):
                do = stages(b)
                if do.A:
                    pe.wait_ge(s.k_scaled, b + 1)
                    pe.wait_ge(s.q_rot, b + 1)
                    if do.C:
                        pe.wait_ge(s.pxT, 4 * (b - 1))
                    tr(qb[0][:, 0:T], kr[:, :], ident[0:T, 0:T]).then_inc(s.kT_ps, 1)
                    for i in range(4):
                        if i == 0 and do.X:
                            pe.wait_ge(s.x1, b)
                        if i == 1 and do.C:
                            pe.wait_ge(s.rank_used, b - 2)
                        if i == 3 and do.C:
                            pe.wait_ge(s.x2, b - 1)
                        for j in range(QH):
                            h = QH * i + j
                            last = tr(wb[i][:, T * j:T * (j + 1)], qr[:, D * h:D * (h + 1)], ident[0:T, 0:T])
                        last.then_inc(s.qT_ps, 1)
                    pe.wait_ge(s.kT, b + 1)
                    for i in range(4):
                        pe.wait_ge(s.qT, 4 * b + i + 1)
                        mm(qb[i][0:T, 0:QW], identb[:, :], mask4[:, :], start=True, stop=False)
                        for j in range(QH):
                            h = QH * i + j
                            last = mm(qb[i][0:T, T * j:T * (j + 1)], T16[:, T * h:T * (h + 1)], kT[:, :],
                                      start=False, stop=j == QH - 1)
                        last.then_inc(s.s_ps, 1)
                if do.X:
                    pe.wait_ge(s.ln2_h, b)
                    to_columns(wb[0], h2).then_inc(s.h2T_ps, 1)
                    pe.wait_ge(s.ld_ctx, 16 * b)
                    for i in range(4):
                        last = mm(wb[2][:, T * i:T * (i + 1)], w_kx[:, P * i:P * (i + 1)], ctxT[:, :],
                                  start=i == 0, stop=True, skip_group_check=True)
                    last.then_inc(s.ck_ps, 1)
                    if do.C:
                        pe.wait_ge(s.x2, b - 1)
                    mm(wb[3][0:T, :], ctxT[:, :], w_kx[:, 512:1024], start=True, stop=True).then_inc(s.cv_ps, 1)
                    pe.wait_ge(s.h2T, b)
                    if do.C:
                        pe.wait_ge(s.rank_used, b - 2)
                    for i in range(4):
                        for k in range(KC):
                            last = mm(wb[1][:, T * i:T * (i + 1)], w_q[:, 512 * k + P * i:512 * k + P * (i + 1)],
                                      h2T[:, T * k:T * (k + 1)], start=k == 0, stop=k == KC - 1)
                    last.then_inc(s.qp_ps, 1)
                if do.Q:
                    ln1_columns(b + 1)
                if do.X:
                    pe.wait_ge(s.s_scaled, 4 * (b + 1) if do.A else 4 * NB)
                    if do.C:
                        pe.wait_ge(s.pxT, 4 * (b - 1))
                    pe.wait_ge(s.ck, b)
                    for j in range(4):
                        mm(qb[j][0:T, 0:QW], identb[:, :], mask4[:, :], start=True, stop=False)
                    pe.wait_ge(s.qp, b)
                    for i in range(4):
                        for j in range(4):
                            r = slice(DX * j, DX * (j + 1))
                            last = mm(qb[j][0:T, T * i:T * (i + 1)], qpT[r, T * i:T * (i + 1)],
                                      ckT[r, T * i:T * (i + 1)], start=False, stop=i == 3)
                    last.then_inc(s.sx_ps, 1)
                if do.Q:
                    compress(b + 1)
                    pe.wait_ge(s.s_scaled, 4 * b + 4)
                    if do.X:
                        pe.wait_ge(s.sx, b)
                    queries(b + 1)
                if do.A:
                    pe.wait_ge(s.p_norm, b + 1)
                    for i in range(4):
                        if i == 2 and do.Q:
                            pe.wait_ge(s.kv, b + 2)
                        if i == 3 and do.X:
                            pe.wait_ge(s.cv, b)
                        for j in range(QH):
                            h = QH * i + j
                            last = tr(wb[i][0:T, T * j:T * (j + 1)], Pm[0:T, T * h:T * (h + 1)], ident[0:T, 0:T])
                        last.then_inc(s.pT_ps, 1)
                    pe.wait_ge(s.v, b + 1)
                    for i in range(4):
                        pe.wait_ge(s.pT, 4 * b + i + 1)
                        mm(wb[i][:, 0:QW], vS[:, :], T16[0:T, QW * i:QW * (i + 1)], start=True, stop=True)\
                            .then_inc(s.o_ps, 1)
                if do.C:
                    if do.A:
                        pe.wait_ge(s.oT, 4 * b + 2)
                    pe.wait_ge(s.rank_used, b - 2)
                    pe.wait_ge(s.ln3_h, b - 1)
                    to_columns(wb[1], h3x).then_inc(s.h3T_ps, 1)
                if do.A:
                    project(b, range(0, 12))
                if do.C:
                    pe.wait_ge(s.h3s, b - 1)
                    for k in range(KC):
                        last = mm(wb[2][0:T, 0:NE], h3s[:, T * k:T * (k + 1)], w_r[:, NE * k:NE * (k + 1)],
                                  start=k == 0, stop=k == KC - 1)
                    last.then_inc(s.lg_ps, 1)
                if do.X:
                    pe.wait_ge(s.px_exp, b)
                    if do.Q:
                        pe.wait_ge(s.q_out, b + 2)
                        pe.wait_ge(s.q_ssq, b + 2)
                    for i in range(4):
                        for j in range(QH):
                            h = QH * i + j
                            last = tr(qb[i][0:T, T * j:T * (j + 1)], PX[0:T, T * h:T * (h + 1)], ident[0:T, 0:T])
                        last.then_inc(s.pxT_ps, 1)
                if do.A:
                    project(b, range(12, 14))
                if do.X:
                    if do.C:
                        pe.wait_ge(s.h3T, b - 1)
                    pe.wait_ge(s.cv, b)
                    for j in range(4):
                        pe.wait_ge(s.pxT, 4 * (b - 1) + j + 1)
                        for i in range(4):
                            h = 4 * i + j
                            last = mm(wb[1][0:T, DX * h:DX * (h + 1)], T16[0:T, T * (4 * j + i):T * (4 * j + i + 1)],
                                      cv[:, DX * h:DX * (h + 1)], start=i == 0 and j == 0, stop=True,
                                      skip_group_check=True)
                    last.then_inc(s.avx_ps, 1)
                if do.A:
                    project(b, range(14, 16)).then_inc(s.x1_ps, 1)
                if do.X:
                    pe.wait_ge(s.ox, b)
                    if do.C:
                        pe.wait_ge(s.lg, b - 1)
                    to_columns(wb[2], ox).then_inc(s.oxT_ps, 1)
                if do.C:
                    pe.wait_ge(s.chosen, b - 1)
                    pe.wait_ge(s.h3T, b - 1)
                    mm(wb[1][0:T, 0:NE], tri[:, :], chosen[:, :], start=True, stop=True)
                    mm(wb[1][0:T, NE:2 * NE], ones[:, :], chosen[:, :], start=True, stop=True).then_inc(s.rank_ps, 1)
                if do.X:
                    pe.wait_ge(s.oxT, b)
                    for k in range(KC):
                        last = mm(wb[3][0:T, :], oxT[:, T * k:T * (k + 1)], w_out[:, 512 * k:512 * (k + 1)],
                                  start=k == 0, stop=k == KC - 1)
                    last.then_inc(s.x2_ps, 1)

            for g in range(G - 1):
                join(g)
            pe.wait_ge(s.ld_const, 16 * 14)
            pe.wait_ge(s.ld_w, 48)
            pe.wait_ge(s.wc, 4 * (G - 1))
            ln1_columns(0)
            compress(0)
            queries(0)
            join(G - 1)
            pe.wait_ge(s.wc, 4 * G)
            pe.wait_ge(s.ld_wx, 64)
            pe.wait_ge(s.h1T, 1)
            pipeline(pe, step)

            pe.wait_ge(s.ld_sh, 48)
            pe.wait_ge(s.x2, NB)
            pe.wait_ge(s.h3T, NB)
            pe.wait_ge(s.rank_used, NB)
            def shared_inner(g):
                for f in range(4):
                    pe.wait_ge(s.sh_act, 4 * g + f - 1) if f >= 2 else pe.wait_ge(s.sh_act, 4 * g)
                    for w, bank, done in ((w_sg, qb[f % 2], s.sh_g), (w_su, qb[2 + f % 2], s.sh_u)):
                        for k in range(KC):
                            last = mm(bank[:, 0:QW], w[:, 512 * k + P * f:512 * k + P * (f + 1)],
                                      h3T[:, bass.ds(g * QW + NTOK * k, QW)], start=k == 0, stop=k == KC - 1)
                        last.then_inc(done, 1)
                pe.wait_ge(s.sh_act, 4 * g + 4)

            def shared_outer(g):
                for t in range(4):
                    pe.wait_ge(s.sh_y, 4 * g)
                    for f in range(4):
                        last = mm(wb[t][0:T, :], shact[:, QW * f + T * t:QW * f + T * (t + 1)],
                                  w_sd[:, 512 * f:512 * (f + 1)], start=f == 0, stop=f == 3)
                    last.then_inc(s.sh_y_ps, 1)

            with pe.Fori(0, 3) as g:
                shared_inner(g)
                shared_outer(g)
            shared_inner(3)
            pe.wait_ge(s.ix_f, 1)
            tr(qb[0][:, 0:2 * NE], ixf, ident[0:2 * NE, 0:2 * NE]).then_inc(s.ix_T, 1)
            shared_outer(3)
            pe.wait_ge(s.idx, 1)

            def x_columns(e, u):
                pe.wait_ge(s.gath[u % 2], 32 * (e // 2 + 1) if isinstance(e, int) else 16 * e + (32 if u % 2 == 0 else 16))
                pe.wait_ge(m.xT, e)
                for j in range(FAST):
                    for k in range(KC):
                        last = tr(QS[:, 256 * k + P * j:256 * k + P * (j + 1)], Xg[u % 2][j][:, P * k:P * (k + 1)], ident[:, :])
                last.then_inc(m.xT_ps, 1)

            x_columns(0, 0)
            with pe.Fori(0, NE // RING) as r:
                e0 = r * RING
                for u in range(RING):
                    e = e0 + u
                    pe.wait_ge(s.ring[u], 8 * e0 + 32)
                    pe.wait_ge(m.xT, e + 1)
                    pe.wait_ge(m.act, e)
                    for f in range(4):
                        for k in range(KC):
                            last = mm(QS[:, 1024 + 256 * f:1280 + 256 * f], w1s[u][:, 512 * k + P * f:512 * k + P * (f + 1)],
                                      XT[u % 2][:, 256 * k:256 * (k + 1)], start=k == 0, stop=k == KC - 1)
                    last.then_inc(m.gu_ps, 1)
                    if u < RING - 1:
                        x_columns(e + 1, u + 1)
                    else:
                        with pe.If(r < NE // RING - 1):
                            x_columns(e + 1, u + 1)
                            pe.nop(nofuse=True)
                    pe.wait_ge(m.act, e + 1)
                    pe.wait_ge(m.y_w, e)
                    for j in range(FAST):
                        for f in range(FE // P):
                            last = mm(wb[j][:, :], ea[:, 256 * f + P * j:256 * f + P * (j + 1)],
                                      w2s[u][:, 512 * f:512 * (f + 1)], start=f == 0, stop=f == FE // P - 1)
                    last.then_inc(m.y_ps, 1)

            done = pe.alloc_register("pe_late")
            pe.reg_mov(done, 0)
            pe.wait_ge(s.cnt, 2)
            longest = pe.value_load(most[0:1, 0:1], min_val=0, max_val=NTOK)
            with pe.If(longest > BLK * FAST):
                with pe.Fori(0, NE) as e:
                    c = pe.value_load(cnt[0:1, bass.ds(e, 1)], min_val=0, max_val=NTOK)
                    with pe.If(c > BLK * FAST):
                        with pe.Fori(FAST, NBLK) as j:
                            with pe.If(c > BLK * j):
                                n = pe.snap(done)
                                pe.wait_ge(m.y_w, NE)
                                pe.wait_ge(o.y_w, n)
                                pe.wait_ge(o.g, 16 * n + 16)
                                for k in range(KC):
                                    last = tr(QS[:, P * k:P * (k + 1)], Xg[0][0][:, P * k:P * (k + 1)], ident[:, :])
                                last.then_inc(o.xT_ps, 1)
                                pe.wait_ge(o.xT, n + 1)
                                pe.wait_ge(o.w, 32 * n + 32)
                                for f in range(4):
                                    for k in range(KC):
                                        last = mm(QS[:, 1024 + P * f:1024 + P * (f + 1)], w1s[0][:, 512 * k + P * f:512 * k + P * (f + 1)],
                                                  XT[0][:, P * k:P * (k + 1)], start=k == 0, stop=k == KC - 1)
                                last.then_inc(o.gu_ps, 1)
                                pe.wait_ge(o.act, n + 1)
                                for f in range(FE // P):
                                    last = mm(wb[0][:, :], ea[:, P * f:P * (f + 1)], w2s[0][:, 512 * f:512 * (f + 1)],
                                              start=f == 0, stop=f == FE // P - 1)
                                last.then_inc(o.y_ps, 1)
                                pe.reg_add(done, done, 1)
                                pe.nop(nofuse=True)
                        pe.nop(nofuse=True)
                pe.nop(nofuse=True)

        @block.scalar
        def _(act):
            fn = nc.scalar.activation

            def copy(dst, src):
                return fn(dst, src, ACT.Copy)

            def joined(heads):
                for n in heads:
                    act.wait_ge(s.wc_ps, n + 1)
                    act.wait_ge(s.wc, n)
                    copy(wc[:, 512 * n:512 * (n + 1)], wb[n % 4]).then_inc(s.wc, 1)

            def ln1_columns(c):
                act.wait_ge(s.h1T_ps, c + 1)
                act.wait_ge(s.kv_ps, c)
                copy(h1T[:, :], wb[0][:, 0:QW]).then_inc(s.h1T, 1)

            def compressed(c):
                act.wait_ge(s.hq_ps, c + 1)
                act.wait_ge(s.q_ps, c)
                copy(hqT[:, :], wb[1][:, 0:T]).then_inc(s.hqT, 1)
                act.wait_ge(s.kv_ps, c + 1)
                act.wait_ge(s.v, c)
                act.wait_ge(s.k_rot, c)
                copy(kvs[:, :], wb[2][0:T, 0:2 * D]).then_inc(s.kv, 1)

            def queries_out(c):
                act.wait_ge(s.q_ps, c + 1)
                act.wait_ge(s.qT_ps, 4 * c)
                copy(qr, QS[0:T, :]).then_inc(s.q_out, 1)

            def squares(c):
                act.wait_ge(s.q_rot, c + 1)
                act.wait_ge(s.k_rot, c + 1)
                act.wait_ge(s.qk_var, c)
                fn(junk[:, :], kr[:, :], ACT.Square, accum_out=ssq[:, NH:NH + 1])
                for h in range(NH):
                    last = fn(QS[0:T, D * h:D * (h + 1)], qr[:, D * h:D * (h + 1)], ACT.Square, accum_out=ssq[:, h:h + 1])
                last.then_inc(s.q_ssq, 1)

            def step(b):
                do = stages(b)
                if do.A:
                    act.wait_ge(s.kT_ps, b + 1)
                    act.wait_ge(s.s_ps, 4 * b)
                    copy(kT[:, :], qb[0][:, 0:T]).then_inc(s.kT, 1)
                    act.wait_ge(s.kv, b + 1)
                    act.wait_ge(s.o_ps, 4 * b)
                    copy(vS[:, :], kvs[:, D:2 * D]).then_inc(s.v, 1)
                    if do.C:
                        act.wait_ge(s.avx_ps, b - 1)
                    for i in range(4):
                        act.wait_ge(s.qT_ps, 4 * b + i + 1)
                        copy(T16[:, QW * i:QW * (i + 1)], wb[i][:, 0:QW]).then_inc(s.qT, 1)
                if do.X:
                    act.wait_ge(s.h2T_ps, b)
                    act.wait_ge(s.qp_ps, b - 1)
                    copy(h2T[:, :], wb[0][:, 0:QW]).then_inc(s.h2T, 1)
                    act.wait_ge(s.ck_ps, b)
                    act.wait_ge(s.sx_ps, b - 1)
                    copy(ckT[:, :], wb[2][:, 0:QW]).then_inc(s.ck, 1)
                    act.wait_ge(s.cv_ps, b)
                    act.wait_ge(s.avx_ps, b - 1)
                    copy(cv[:, :], wb[3][0:T, :]).then_inc(s.cv, 1)
                    act.wait_ge(s.qp_ps, b)
                    copy(qpT[:, :], wb[1][:, 0:QW]).then_inc(s.qp, 1)
                if do.Q:
                    ln1_columns(b + 1)
                if do.A:
                    act.wait_ge(s.s_shift, b + 1)
                    fn(Pm[0:T, :], Pm[0:T, :], ACT.Exp).then_inc(s.p_exp, 1)
                    act.wait_ge(s.s_sink, b + 1)
                    act.wait_ge(s.p_den, b)
                    fn(esink[:, :], sdiff[:, :], ACT.Exp).then_inc(s.e_sink, 1)
                if do.X:
                    act.wait_ge(s.sx_ps, b)
                    act.wait_ge(s.pxT_ps, 4 * (b - 1))
                    fn(PX[0:T, :].rearrange("t (a n) -> t a n", a=4),
                       QS[0:T, :].rearrange("t (a n) -> t a n", a=4)[:, :, 0:QW], ACT.Copy,
                       scale=DX ** -0.5).then_inc(s.sx, 1)
                if do.Q:
                    compressed(b + 1)
                    queries_out(b + 1)
                if do.A:
                    act.wait_ge(s.s_ps, 4 * b + 4)
                    for i in range(4):
                        act.wait_ge(s.pT_ps, 4 * b + i + 1)
                        copy(T16[0:T, QW * i:QW * (i + 1)], wb[i][0:T, 0:QW]).then_inc(s.pT, 1)
                    act.wait_ge(s.x1_ps, b)
                    for i in range(4):
                        act.wait_ge(s.o_ps, 4 * b + i + 1)
                        copy(OT[:, QW * i:QW * (i + 1)], wb[i][:, 0:QW]).then_inc(s.oT, 1)
                if do.C:
                    act.wait_ge(s.h3T_ps, b - 1)
                    act.wait_ge(s.lg_ps, b - 2)
                    copy(h3s[:, :], wb[1][:, 0:QW]).then_inc(s.h3s, 1)
                    copy(h3T[:, :].rearrange("p (k n) -> p k n", k=KC)[:, :, bass.ds(T * (b - 2), T)],
                         wb[1][:, 0:QW].rearrange("p (k n) -> p k n", k=KC)).then_inc(s.h3T, 1)
                if do.X:
                    act.wait_ge(s.sx_shift, b)
                    fn(PX[0:T, :], PX[0:T, :], ACT.Exp).then_inc(s.px_exp, 1)
                if do.Q:
                    squares(b + 1)
                if do.C:
                    act.wait_ge(s.topd, b - 1)
                    act.wait_ge(s.top_w, b - 2)
                    fn(e4[:, :], d4[:, :], ACT.Exp, accum_out=sum4[:, :]).then_inc(s.top_exp, 1)
                if do.X:
                    if do.A:
                        act.wait_ge(s.o_ps, 4 * b + 4)
                    else:
                        act.wait_ge(s.avx_ps, b - 1)
                    for i in range(4):
                        act.wait_ge(s.pxT_ps, 4 * (b - 1) + i + 1)
                        copy(T16[0:T, QW * i:QW * (i + 1)], qb[i][0:T, 0:QW]).then_inc(s.pxT, 1)
                    act.wait_ge(s.oxT_ps, b)
                    act.wait_ge(s.x2_ps, b - 1)
                    copy(oxT[:, :], wb[2][:, 0:QW]).then_inc(s.oxT, 1)

            joined(range(0, 12, 2))
            ln1_columns(0)
            compressed(0)
            queries_out(0)
            joined(range(12, 16, 2))
            squares(0)
            pipeline(act, step)

            with act.Fori(0, 4) as g:
                for f in range(4):
                    act.wait_ge(s.sh_g, 4 * g + f + 1)
                    act.wait_ge(s.sh_act, 4 * g + f)
                    fn(shtmp[:, :], qb[f % 2][:, 0:QW], ACT.Silu).then_inc(s.sh_silu, 1)

            with act.Fori(0, NE // RING) as r:
                e0 = r * RING
                for u in range(RING):
                    act.wait_ge(m.gu_ps, e0 + u + 1)
                    act.wait_ge(m.act, e0 + u)
                    fn(et, QS[:, 1024:1536], ACT.Silu).then_inc(m.act_s, 1)
                    act.wait_ge(m.y_ps, e0 + u + 1)
                    act.wait_ge(m.wcol, FAST * (e0 + u) + FAST)
                    act.wait_ge(m.scat_add, 32 * e0 + 32 * max(u - 1, 0))
                    for j in range(FAST):
                        last = fn(Y[u % 2][:, 512 * j:512 * (j + 1)], wb[j][:, :], ACT.Copy,
                                  scale=wcol[u][:, j:j + 1])
                    last.then_inc(m.y_w, 1)

            done = act.alloc_register("act_late")
            act.reg_mov(done, 0)
            act.wait_ge(s.cnt, 2)
            longest = act.value_load(most[0:1, 0:1], min_val=0, max_val=NTOK)
            with act.If(longest > BLK * FAST):
                with act.Fori(0, NE) as e:
                    c = act.value_load(cnt[0:1, bass.ds(e, 1)], min_val=0, max_val=NTOK)
                    with act.If(c > BLK * FAST):
                        with act.Fori(FAST, NBLK) as j:
                            with act.If(c > BLK * j):
                                n = act.snap(done)
                                act.wait_ge(o.gu_ps, n + 1)
                                fn(et[:, 0:256], QS[:, 1024:1280], ACT.Silu).then_inc(o.act_s, 1)
                                act.wait_ge(o.y_ps, n + 1)
                                act.wait_ge(m.scat_add, 32 * NE)
                                act.wait_ge(o.add, 16 * n)
                                fn(Y[0][:, 0:512], wb[0][:, :], ACT.Copy, scale=Xg[0][0][:, bass.ds(HID + e, 1)]).then_inc(o.y_w, 1)
                                act.reg_add(done, done, 1)
                                act.nop(nofuse=True)
                        act.nop(nofuse=True)
                act.nop(nofuse=True)

        @block.vector
        def _(dve):
            tt, ts, red = nc.vector.tensor_tensor, nc.vector.tensor_scalar, nc.vector.tensor_reduce

            def per_head(v, n, w=T):
                return v.unsqueeze(2).to_broadcast([T, n, w])

            nc.vector.memset(phalf[:, :], -0.5).then_inc(s.wqk, 1)
            dve.wait_ge(s.ld_const, 16 * 14)
            nc.vector.scalar_tensor_tensor(out=wqk[:, :], in0=wqk[:, :], scalar=math.sqrt(D), in1=wkn[:, :],
                                           op0=ALU.mult, op1=ALU.mult).then_inc(s.wqk, 1)
            nc.vector.tensor_copy(run[:, :], runs[:, :]).then_inc(s.wqk, 1)
            dve.wait_ge(s.wqk, 3)
            def joined(heads):
                for n in heads:
                    dve.wait_ge(s.wc_ps, n + 1)
                    dve.wait_ge(s.wc, n)
                    nc.vector.tensor_copy(wc[:, 512 * n:512 * (n + 1)], wb[n % 4]).then_inc(s.wc, 1)

            def row(c):
                return resid[:, bass.ds(HID * c, HID)]

            def ln_stats(k, c, stats, aggr, done):
                nc.vector.bn_stats(st[k][:, :], row(c)).then_inc(stats, 1)
                wait_alone(dve, stats, c + 1)
                nc.vector.bn_aggr(mv[k][:, :], st[k][:, :]).then_inc(aggr, 1)
                dve.wait_ge(aggr, c + 1)
                ts(var[k][:, 0:1], mv[k][:, 1:2], 1e-5, None, ALU.add).then_inc(done, 1)

            def ln1_apply(c):
                dve.wait_ge(s.ln1_rstd, c + 1)
                dve.wait_ge(s.h1T_ps, c)
                ts(h1, row(c), mv[0][:, 0:1], rstd[0][:, 0:1], ALU.subtract, ALU.mult).then_inc(s.ln1_h, 1)

            def rotate(c):
                r3 = qr.rearrange("t (h d) -> t h d", d=D)
                t3 = rtmp.rearrange("t (h d) -> t h d", d=RD)
                hr = RD // 2
                dve.wait_ge(s.kv, c + 1)
                dve.wait_ge(s.kT_ps, c)
                tt(kr[:, 0:RD], kvs[:, 0:RD], c64[:, :], ALU.mult).then_inc(s.k_parts, 1)
                tt(ktmp[:, 0:hr], kvs[:, hr:RD], s64[:, 0:hr], ALU.mult).then_inc(s.k_parts, 1)
                tt(ktmp[:, hr:RD], kvs[:, 0:hr], s64[:, hr:RD], ALU.mult).then_inc(s.k_parts, 1)
                nc.vector.tensor_copy(kr[:, RD:D], kvs[:, RD:D])
                dve.wait_ge(s.k_parts, 3 * c + 3)
                tt(kr[:, 0:RD], kr[:, 0:RD], ktmp[:, :], ALU.add).then_inc(s.k_rot, 1)
                dve.wait_ge(s.q_out, c + 1)
                tt(t3[:, :, 0:hr], r3[:, :, hr:RD], s64[:, 0:hr].unsqueeze(1).to_broadcast([T, NH, hr]), ALU.mult)\
                    .then_inc(s.q_parts, 1)
                tt(t3[:, :, hr:RD], r3[:, :, 0:hr], s64[:, hr:RD].unsqueeze(1).to_broadcast([T, NH, hr]), ALU.mult)\
                    .then_inc(s.q_parts, 1)
                dve.wait_ge(s.q_parts, 3 * c + 2)
                tt(r3[:, :, 0:RD], r3[:, :, 0:RD], c64[:, :].unsqueeze(1).to_broadcast([T, NH, RD]), ALU.mult)\
                    .then_inc(s.q_parts, 1)
                dve.wait_ge(s.q_parts, 3 * c + 3)
                tt(r3[:, :, 0:RD], r3[:, :, 0:RD], t3, ALU.add).then_inc(s.q_rot, 1)

            def norms(c):
                dve.wait_ge(s.q_ssq, c + 1)
                dve.wait_ge(s.qk_rstd, c)
                ts(qkv_var[:, :], ssq[:, :], D * 1e-6, None, ALU.add).then_inc(s.qk_var, 1)

            def scale_keys(c):
                dve.wait_ge(s.k_rot, c + 1)
                dve.wait_ge(s.qk_rstd, c + 1)
                nc.vector.scalar_tensor_tensor(out=kr[:, :], in0=kr[:, :], scalar=rall[:, NH:NH + 1], in1=wqk[:, :],
                                               op0=ALU.mult, op1=ALU.mult).then_inc(s.k_scaled, 1)

            def step(b):
                do = stages(b)
                if do.Q:
                    if isinstance(b, int) and b == 0:
                        dve.wait_ge(s.ld_x, 16)
                    ln_stats(0, b + 1, s.ln1_stats, s.ln1_mv, s.ln1_var)
                if do.A:
                    dve.wait_ge(s.qk_rstd, b + 1)
                    dve.wait_ge(s.pT_ps, 4 * b)
                    for i in range(4):
                        dve.wait_ge(s.s_ps, 4 * b + i + 1)
                        tt(Pm[0:T, QW * i:QW * (i + 1)].rearrange("t (h n) -> t h n", n=T),
                           qb[i][0:T, 0:QW].rearrange("t (h n) -> t h n", n=T),
                           per_head(rall[:, QH * i:QH * (i + 1)], QH), ALU.mult).then_inc(s.s_scaled, 1)
                P3 = Pm[0:T, :].rearrange("t (h n) -> t h n", n=T)
                X3 = PX[0:T, :].rearrange("t (h n) -> t h n", n=T)
                if do.A:
                    dve.wait_ge(s.s_scaled, 4 * b + 4)
                    red(mx[:, :], P3, AX.X, ALU.max).then_inc(s.s_max, 1)
                    dve.wait_ge(s.s_max, b + 1)
                    tt(mx[:, :], mx[:, :], sink[:, :], ALU.max).then_inc(s.s_top, 1)
                if do.Q:
                    ln1_apply(b + 1)
                if do.A:
                    dve.wait_ge(s.s_top, b + 1)
                    tt(P3, P3, per_head(mx[:, :], NH), ALU.subtract).then_inc(s.s_shift, 1)
                    tt(sdiff[:, :], sink[:, :], mx[:, :], ALU.subtract).then_inc(s.s_sink, 1)
                if do.C:
                    c = b - 2
                    dve.wait_ge(s.ln3_rstd, c + 1)
                    ts(xc, row(c), mv[2][:, 0:1], None, ALU.subtract).then_inc(s.ln3_xc, 1)
                    dve.wait_ge(s.ln3_xc, c + 1)
                    dve.wait_ge(s.h3T_ps, c)
                    dve.wait_ge(s.hx_st, 16 * c)
                    nc.vector.scalar_tensor_tensor(out=h3x[:, 0:HID], in0=xc, scalar=rstd[2][:, 1:2], in1=normw[:, :],
                                                   op0=ALU.mult, op1=ALU.mult).then_inc(s.ln3_h, 1)
                    nc.vector.scalar_tensor_tensor(out=row(c), in0=xc, scalar=rstd[2][:, 0:1], in1=row(c),
                                                   op0=ALU.mult, op1=ALU.add).then_inc(s.ln3_base, 1)
                if do.A:
                    dve.wait_ge(s.p_exp, b + 1)
                    red(den[:, :], P3, AX.X, ALU.add).then_inc(s.p_sum, 1)
                    dve.wait_ge(s.p_sum, b + 1)
                    dve.wait_ge(s.e_sink, b + 1)
                    tt(den[:, :], den[:, :], esink[:, :], ALU.add).then_inc(s.p_den, 1)
                    dve.wait_ge(s.p_den, b + 1)
                    nc.vector.reciprocal(rinv[:, :], den[:, :]).then_inc(s.p_inv, 1)
                    dve.wait_ge(s.p_inv, b + 1)
                    tt(P3, P3, per_head(rinv[:, :], NH), ALU.mult).then_inc(s.p_norm, 1)
                if do.X:
                    dve.wait_ge(s.sx, b)
                    red(mxx[:, :], X3, AX.X, ALU.max).then_inc(s.sx_max, 1)
                    dve.wait_ge(s.sx_max, b)
                    tt(X3, X3, per_head(mxx[:, :], NX), ALU.subtract).then_inc(s.sx_shift, 1)
                if do.Q:
                    rotate(b + 1)
                if do.X:
                    dve.wait_ge(s.px_exp, b)
                    red(denx[:, :], X3, AX.X, ALU.add).then_inc(s.px_sum, 1)
                    dve.wait_ge(s.px_sum, b)
                    nc.vector.reciprocal(rx[:, :], denx[:, :]).then_inc(s.px_inv, 1)
                if do.C:
                    c = b - 2
                    dve.wait_ge(s.lg_ps, c + 1)
                    nc.vector.tensor_copy(lgs[:, :], wb[2][0:T, 0:NE]).then_inc(s.lg, 1)
                    wait_alone(dve, s.lg, c + 1)
                    nc.vector.max(v8[:, :], lgs[:, :]).then_inc(s.top8, 1)
                    dve.wait_ge(s.top8, c + 1)
                    ts(d4[:, :], v8[:, 0:TOPK], v8[:, 0:1], None, ALU.subtract).then_inc(s.topd, 1)
                    nc.vector.max_index(i8[:, :], v8[:, :], lgs[:, :]).then_inc(s.topi, 1)
                    dve.wait_ge(s.topi, 2 * c + 1)
                    nc.vector.tensor_copy(idxf[:, :], i8[:, 0:TOPK]).then_inc(s.topi, 1)
                    dve.wait_ge(s.topi, 2 * c + 2)
                    oh3, ow3, pk3 = (t[:, :].rearrange("t (k e) -> t k e", e=NE) for t in (oh, ohw, pick))
                    tt(oh3, eid[:, :].rearrange("t (k e) -> t k e", e=NE), per_head(idxf[:, :], TOPK, NE),
                       ALU.is_equal).then_inc(s.onehot, 1)
                    dve.wait_ge(s.onehot, c + 1)
                    dve.wait_ge(s.rank_ps, c)
                    with nc.allow_low_precision(reason="sums of zeros and one"):
                        red(chosen[:, :], oh[:, :].rearrange("t (k e) -> t e k", e=NE), AX.X, ALU.add)\
                            .then_inc(s.chosen, 1)
                    dve.wait_ge(s.top_exp, c + 1)
                    nc.vector.reciprocal(inv4[:, :], sum4[:, :]).then_inc(s.top_inv, 1)
                    dve.wait_ge(s.top_inv, c + 1)
                    ts(w4[:, :], e4[:, :], inv4[:, 0:1], None, ALU.mult).then_inc(s.top_w, 1)
                    dve.wait_ge(s.top_w, c + 1)
                    tt(ow3, oh3, per_head(w4[:, :], TOPK, NE), ALU.mult).then_inc(s.ohw, 1)
                    dve.wait_ge(s.ohw, c + 1)
                    red(h3x[:, HID:HXW], ohw[:, :].rearrange("t (k e) -> t e k", e=NE), AX.X, ALU.add).then_inc(s.wd, 1)
                if do.Q:
                    norms(b + 1)
                if do.X:
                    dve.wait_ge(s.px_inv, b)
                    dve.wait_ge(s.avx_ps, b)
                    dve.wait_ge(s.oxT_ps, b - 1)
                    tt(ox[:, :].rearrange("t (i j d) -> t i j d", i=4, j=4),
                       wb[1][0:T, :].rearrange("t (i j d) -> t i j d", i=4, j=4),
                       rx[:, :].rearrange("t (j i) -> t i j", i=4).unsqueeze(3).to_broadcast([T, 4, 4, DX]),
                       ALU.mult).then_inc(s.ox, 1)
                if do.A:
                    dve.wait_ge(s.x1_ps, b + 1)
                    tt(row(b), row(b), wb[0][0:T, :], ALU.add).then_inc(s.x1, 1)
                    wait_alone(dve, s.x1, b + 1)
                    ln_stats(1, b, s.ln2_stats, s.ln2_mv, s.ln2_var)
                if do.Q:
                    scale_keys(b + 1)
                if do.C:
                    c = b - 2
                    dve.wait_ge(s.rank_ps, c + 1)
                    tt(rk[:, :], wb[1][0:T, 0:NE], run[:, :], ALU.add).then_inc(s.rank, 1)
                    dve.wait_ge(s.rank, c + 1)
                    tt(run[:, :], wb[1][0:T, NE:2 * NE], run[:, :], ALU.add).then_inc(s.rank_used, 1)
                    tt(pick[:, :].rearrange("t (k e) -> t k e", e=NE), oh[:, :].rearrange("t (k e) -> t k e", e=NE),
                       rk[:, :].unsqueeze(1).to_broadcast([T, TOPK, NE]), ALU.mult).then_inc(s.picked, 1)
                    dve.wait_ge(s.picked, c + 1)
                    dve.wait_ge(s.rank_used, c + 1)
                    dve.wait_ge(s.scat, 64 * c)
                    with nc.allow_low_precision(reason="whole numbers under 2^24"):
                        red(slot[:, :], pick[:, :].rearrange("t (k e) -> t k e", e=NE), AX.X, ALU.add)\
                            .then_inc(s.slots, 1)
                    nc.vector.tensor_copy(tok[:, :], tokall[:, bass.ds(c, 1)]).then_inc(s.slots, 1)
                if do.A:
                    dve.wait_ge(s.ln2_rstd, b + 1)
                    dve.wait_ge(s.h2T_ps, b)
                    ts(h2, row(b), mv[1][:, 0:1], rstd[1][:, 0:1], ALU.subtract, ALU.mult).then_inc(s.ln2_h, 1)
                if do.X:
                    c = b - 1
                    dve.wait_ge(s.x2_ps, c + 1)
                    tt(row(c), row(c), wb[3][0:T, :], ALU.add).then_inc(s.x2, 1)
                    wait_alone(dve, s.x2, c + 1)
                    nc.vector.bn_stats(st[2][:, :], row(c)).then_inc(s.ln3_stats, 1)
                    wait_alone(dve, s.ln3_stats, c + 1)
                    nc.vector.bn_aggr(mv[2][:, :], st[2][:, :]).then_inc(s.ln3_mv, 1)
                    dve.wait_ge(s.ln3_mv, c + 1)
                    ts(var[2][:, 0:1], mv[2][:, 1:2], 1e-5, None, ALU.add).then_inc(s.ln3_g, 1)
                    ts(var[2][:, 1:2], mv[2][:, 1:2], 1.0 + 1e-6, 1e-11, ALU.mult, ALU.add).then_inc(s.ln3_var, 1)

            wait_alone(dve, s.ld_x0, 16)
            ln_stats(0, 0, s.ln1_stats, s.ln1_mv, s.ln1_var)
            ln1_apply(0)
            joined(range(1, 12, 2))
            rotate(0)
            joined(range(13, 16, 2))
            norms(0)
            scale_keys(0)
            pipeline(dve, step)

            tt(rk[0:1, :], run[0:1, :], runs[0:1, :], ALU.subtract).then_inc(s.cnt_f, 1)
            dve.wait_ge(s.cnt_f, 1)
            nc.vector.tensor_copy(cnt[:, :], rk[0:1, :]).then_inc(s.cnt, 1)
            with nc.allow_low_precision(reason="whole numbers under 2^24"):
                red(most[:, :], rk[0:1, :], AX.X, ALU.max).then_inc(s.cnt, 1)

            dve.wait_ge(s.ln3_base, NB)
            def shared_inner(g):
                for f in range(4):
                    dve.wait_ge(s.sh_silu, 4 * g + f + 1)
                    dve.wait_ge(s.sh_u, 4 * g + f + 1)
                    dve.wait_ge(s.sh_y_ps, 4 * g)
                    tt(shact[:, QW * f:QW * (f + 1)], shtmp[:, :], qb[2 + f % 2][:, 0:QW], ALU.mult).then_inc(s.sh_act, 1)

            def shared_rows(g):
                for t in range(4):
                    dve.wait_ge(s.sh_y_ps, 4 * g + t + 1)
                    dve.wait_ge((s.sh_st0, s.sh_st1)[t % 2], 32 * g + 16 * (t // 2))
                    tt(ytile[t % 2][:, :], resid[:, bass.ds(4 * HID * g + HID * t, HID)], wb[t][0:T, :], ALU.add)\
                        .then_inc(s.sh_y, 1)

            with dve.Fori(0, 3) as g:
                shared_inner(g)
                shared_rows(g)
            dve.wait_ge(s.ix_ld, 16 * FAST)
            nc.vector.tensor_copy(ixf, ixr).then_inc(s.ix_f, 1)
            shared_inner(3)
            dve.wait_ge(s.ix_T, 1)
            nc.vector.tensor_copy(idx[:, :], qb[0][:, 0:2 * NE]).then_inc(s.idx, 1)
            shared_rows(3)

            def x_columns(e, u):
                dve.wait_ge(m.xT_ps, e + 1)
                for j in range(FAST):
                    nc.vector.tensor_copy(wcol[u][:, j:j + 1], Xg[u % 2][j][:, bass.ds(HID + e, 1)]).then_inc(m.wcol, 1)
                dve.wait_ge(m.gu_ps, e)
                nc.vector.tensor_copy(XT[u % 2], QS[:, 0:1024]).then_inc(m.xT, 1)

            with dve.Fori(0, NE // RING) as r:
                e0 = r * RING
                for u in range(RING):
                    x_columns(e0 + u, u)
                    dve.wait_ge(m.act_s, e0 + u + 1)
                    dve.wait_ge(m.y_ps, e0 + u)
                    tt(ea, et, QS[:, 1536:2048], ALU.mult).then_inc(m.act, 1)

            done = dve.alloc_register("dve_late")
            dve.reg_mov(done, 0)
            dve.wait_ge(s.cnt, 2)
            longest = dve.value_load(most[0:1, 0:1], min_val=0, max_val=NTOK)
            with dve.If(longest > BLK * FAST):
                with dve.Fori(0, NE) as e:
                    c = dve.value_load(cnt[0:1, bass.ds(e, 1)], min_val=0, max_val=NTOK)
                    with dve.If(c > BLK * FAST):
                        with dve.Fori(FAST, NBLK) as j:
                            with dve.If(c > BLK * j):
                                n = dve.snap(done)
                                dve.wait_ge(o.xT_ps, n + 1)
                                nc.vector.tensor_copy(XT[0][:, 0:512], QS[:, 0:512]).then_inc(o.xT, 1)
                                dve.wait_ge(o.act_s, n + 1)
                                tt(ea[:, 0:256], et[:, 0:256], QS[:, 1280:1536], ALU.mult).then_inc(o.act, 1)
                                dve.reg_add(done, done, 1)
                                dve.nop(nofuse=True)
                        dve.nop(nofuse=True)
                dve.nop(nofuse=True)

        @block.gpsimd
        def _(pool):
            def power(dst, src):
                return nc.gpsimd.tensor_tensor(out=dst, in0=src, in1=phalf[:, 0:src.shape[1]], op=ALU.pow)

            def on_rows(ap):
                return bass.IndirectOffsetOnAxis(ap, 0)

            def ln1(c):
                pool.wait_ge(s.ln1_var, c + 1)
                power(rstd[0][:, 0:1], var[0][:, 0:1]).then_inc(s.ln1_rstd, 1)

            def qk(c):
                pool.wait_ge(s.qk_var, c + 1)
                pool.wait_ge(s.s_scaled, 4 * c)
                power(rall[:, :], qkv_var[:, :]).then_inc(s.qk_rstd, 1)

            def step(b):
                do = stages(b)
                if do.Q:
                    ln1(b + 1)
                    qk(b + 1)
                if do.A:
                    pool.wait_ge(s.ln2_var, b + 1)
                    power(rstd[1][:, 0:1], var[1][:, 0:1]).then_inc(s.ln2_rstd, 1)
                if do.X:
                    pool.wait_ge(s.ln3_g, b)
                    pool.wait_ge(s.ln3_var, b)
                    power(rstd[2][:, :], var[2][:, :]).then_inc(s.ln3_rstd, 1)
                if do.C:
                    wait_alone(pool, s.slots, 2 * (b - 1))
                    for k in range(TOPK):
                        nc.gpsimd.indirect_dma_start(table, on_rows(slot[:, k:k + 1]), tok[:, :], None)\
                            .then_inc(s.scat, 16)

            wait_alone(pool, s.wqk, 1)
            ln1(0)
            qk(0)
            pool.wait_ge(s.pad_st, 48)
            pipeline(pool, step)

            pool.wait_ge(s.scat, 64 * NB)
            for j in range(FAST):
                pool.dma_start(ixr[NE * j:NE * (j + 1), :],
                               table.rearrange("(e n) o -> e (n o)", e=NE)[:, BLK * j:BLK * (j + 1)]).then_inc(s.ix_ld, 16)
            def shared_rows(g):
                for t in range(4):
                    dst = out[bass.ds(4 * T * g + T * t, T), :]
                    pool.wait_ge(s.sh_y, 4 * g + t + 1)
                    pool.dma_start(dst, ytile[t % 2][:, :]).then_inc((s.sh_st0, s.sh_st1)[t % 2], 16)

            with pool.Fori(0, 3) as g:
                shared_rows(g)

            def gather(e, u, first=False):
                if not first:
                    if not isinstance(e, int):
                        pool.wait_ge(m.scat_add, 32 * (e - 3))
                    pool.wait_ge(m.xT, e - 1)
                    pool.wait_ge(m.wcol, FAST * (e - 1))
                nc.gpsimd.tensor_copy(ixs[u][:, :], idx[:, :].rearrange("p (j e) -> p j e", j=FAST)[:, :, bass.ds(e, 1)]
                                      .rearrange("p j e -> p (j e)")).then_inc(m.ix, 1)
                wait_alone(pool, m.ix, e + 1)
                for j in range(FAST):
                    nc.gpsimd.indirect_dma_start(Xg[u % 2][j], None, hx, on_rows(ixs[u][:, j:j + 1])).then_inc(s.gath[u % 2], 16)

            def scatter(e, u):
                pool.wait_ge(m.y_w, e + 1)
                wait_alone(pool, m.scat_add, 32 * e)
                for j in range(FAST):
                    nc.gpsimd.indirect_dma_start(out, on_rows(ixs[u][:, j:j + 1]), Y[u % 2][:, 512 * j:512 * (j + 1)], None,
                                                 compute_op=ALU.add).then_inc(m.scat_add, 16)

            pool.wait_ge(s.idx, 1)
            pool.wait_ge(s.hx_st, 16 * NB)
            gather(0, 0, first=True)
            gather(1, 1, first=True)
            shared_rows(3)
            pool.wait_ge(s.sh_st0, 8 * NB)
            pool.wait_ge(s.sh_st1, 8 * NB)
            for e in range(2):
                gather(e + 2, e + 2)
                scatter(e, e)
            with pool.Fori(0, NE // RING - 1) as r:
                for u in range(RING):
                    e = r * RING + u + 2
                    gather(e + 2, u)
                    scatter(e, (u + 2) % RING)
            for e in range(NE - 2, NE):
                scatter(e, e % RING)
            pool.wait_ge(m.scat_add, 32 * NE)

            done = pool.alloc_register("pool_late")
            pool.reg_mov(done, 0)
            pool.wait_ge(s.cnt, 2)
            longest = pool.value_load(most[0:1, 0:1], min_val=0, max_val=NTOK)
            with pool.If(longest > BLK * FAST):
                with pool.Fori(0, NE) as e:
                    c = pool.value_load(cnt[0:1, bass.ds(e, 1)], min_val=0, max_val=NTOK)
                    with pool.If(c > BLK * FAST):
                        with pool.Fori(FAST, NBLK) as j:
                            with pool.If(c > BLK * j):
                                n = pool.snap(done)
                                wait_alone(pool, o.idx, 16 * n + 16)
                                nc.gpsimd.indirect_dma_start(Xg[0][0], None, hx, on_rows(oidx)).then_inc(o.g, 16)
                                wait_alone(pool, o.y_w, n + 1)
                                nc.gpsimd.indirect_dma_start(out, on_rows(oidx), Y[0][:, 0:512], None,
                                                             compute_op=ALU.add).then_inc(o.add, 16)
                                pool.wait_ge(o.add, 16 * n + 16)
                                pool.reg_add(done, done, 1)
                                pool.nop(nofuse=True)
                        pool.nop(nofuse=True)
                pool.nop(nofuse=True)

def kernel(**inputs):
    import numpy as np
    import concourse.bacc as bacc
    from concourse.bass_utils import run_bass_kernel_spmd

    np_bf16 = mybir.dt.np(bf16)
    f = {k: np.asarray(v) for k, v in inputs.items()}
    L = "L0_attn_"
    rep = lambda v: np.ascontiguousarray(np.broadcast_to(v[None, :], (T, v.shape[0])))
    arrays = {
        "x": f["x"],
        "ctxT": f["ctx_512"].transpose(0, 2, 1),
        "wq_comp": f[L + "wq_comp"], "wq_up": f[L + "wq_up"],
        "wkv": np.concatenate([f[L + "wk"], f[L + "wv"]], axis=1),
        "qn": rep(f[L + "q_norm_w"]), "kn": rep(f[L + "k_norm_w"]), "sink": rep(f[L + "sink_logit"]),
        "w1T": f[L + "out_w1"].transpose(0, 2, 1), "out_w2": f[L + "out_w2"],
        "WqT": f["L0_xattn_Wq"].T, "WkvT": f["L0_xattn_Wkv_expand"].T, "WoutT": f["L0_xattn_Wout"].T,
        "normw": rep(f["L0_ffn_norm_w"]), "routerT": f["L0_ffn_router_w"].T,
        "w1": f["L0_ffn_w1"], "w2": f["L0_ffn_w2"], "sg": f["L0_ffn_sg"], "su": f["L0_ffn_su"], "sd": f["L0_ffn_sd"],
    }
    inv = np.float32(1.0) / np.float32(10000.0) ** (np.arange(0, RD, 2, dtype=np.float32) / np.float32(RD))
    ang = (np.arange(T, dtype=np.float32)[:, None] * inv[None, :]).astype(np.float64)
    cos, sin = np.cos(ang).astype(np.float32), np.sin(ang).astype(np.float32)
    t = np.arange(T)
    causal = np.where(t[None, :] <= t[:, None], 0.0, NEG).astype(np_bf16)
    arrays |= {
        "c_ident": np.eye(P, dtype=np.float32),
        "c_cos": np.concatenate([cos, cos], axis=1), "c_sin": np.concatenate([-sin, sin], axis=1),
        "c_eid": np.tile(np.arange(NE, dtype=np.float32), (T, TOPK)),
        "c_runs": np.tile(CAP * np.arange(NE, dtype=np.float32), (T, 1)),
        "c_tok": (t[:, None] + T * np.arange(NB)[None, :]).astype(np.int32),
        "c_identb": np.eye(T, dtype=np.float32).astype(np_bf16),
        "c_mask": np.tile(causal, (1, QH)),
        "c_tri": (t[:, None] < t[None, :]).astype(np_bf16),
        "c_ones": np.ones((T, T), dtype=np_bf16),
        "c_table": (NTOK + np.arange(NE * CAP) % PADS).astype(np.int32).reshape(-1, 1),
        "c_zero": np.zeros((PADS, HXW), dtype=np.float32),
    }
    nc = bacc.Bacc("TRN2", target_bir_lowering=False, num_devices=1)
    arrays = {f"in_{k}": np.ascontiguousarray(v) for k, v in arrays.items()}
    aps = {k[3:]: nc.dram_tensor(k, v.shape, mybir.dt.from_np(v.dtype), kind="ExternalInput").ap()
           for k, v in arrays.items()}
    out = nc.dram_tensor("out_rows", (ROWS, HID), fp32, kind="ExternalOutput").ap()
    build(nc, aps, out)
    r = run_bass_kernel_spmd(nc, [arrays], core_ids=[0])
    return r.results[0]["out_rows"][0:NTOK].reshape(NB, T, HID)
```

```python
import math
from contextlib import ExitStack

import concourse.bass as bass
from concourse import mybir

NB, T, HID = 16, 100, 512
NH, D = 16, 128
RD = 64
NX, DX = 16, 32
G, GI = 4, 512
NE, TOPK, FE = 32, 4, 256
FS = 512
P = 128
KC = HID // P
NTOK = NB * T
QH = 4
QW = QH * T
BLK = 128
FAST = 2
NBLK = -(-NTOK // BLK)
CAP = NBLK * BLK
PADS = FAST * BLK
ROWS = NTOK + PADS
HXW = HID + NE
AHEAD = 3
RING = 4
WX = KC * 2 * FE + (FE // P) * HID
NEG = -1e30

fp32, bf16 = mybir.dt.float32, mybir.dt.bfloat16
f32r = mybir.dt.float32r
i32, u32 = mybir.dt.int32, mybir.dt.uint32
ALU, ACT, AX = mybir.AluOpType, mybir.ActivationFunctionType, mybir.AxisListType

class Signals:
    def __init__(self, new):
        self.ld_x0, self.ld_x, self.ld_const, self.ld_w, self.ld_wx, self.ld_half0 = new("ld_x0 ld_x ld_const ld_w ld_wx ld_half0")
        self.ld_half1, self.ld_ctx, self.ld_sh, self.wqk, self.passed = new("ld_half1 ld_ctx ld_sh wqk passed")
        self.wc_ps, self.wc = new("wc_ps wc")
        self.ln1_stats, self.ln1_var, self.ln1_rstd, self.ln1_h, self.ln2_stats = new("ln1_stats ln1_var ln1_rstd ln1_h ln2_stats")
        self.ln2_var, self.ln2_rstd, self.ln2_h = new("ln2_var ln2_rstd ln2_h")
        self.ln3_stats, self.ln3_var, self.ln3_rstd, self.ln3_xc, self.ln3_g = new("ln3_stats ln3_var ln3_rstd ln3_xc ln3_g")
        self.ln3_h, self.ln3_base = new("ln3_h ln3_base")
        self.h1T_ps, self.h1T, self.hq_ps, self.hqT, self.kv_ps, self.kv = new("h1T_ps h1T hq_ps hqT kv_ps kv")
        self.v, self.q_ps, self.q_out, self.q_parts, self.q_rot, self.q_ssq = new("v q_ps q_out q_parts q_rot q_ssq")
        self.qk_var, self.qk_rstd = new("qk_var qk_rstd")
        self.k_parts, self.k_rot, self.k_scaled, self.kT_ps, self.kT, self.qT_ps = new("k_parts k_rot k_scaled kT_ps kT qT_ps")
        self.qT = new("qT")[0]
        self.s_ps, self.s_scaled, self.s_max, self.s_shift, self.s_sink = new("s_ps s_scaled s_max s_shift s_sink")
        self.p_exp, self.e_sink, self.p_sum, self.p_den, self.p_inv, self.p_norm = new("p_exp e_sink p_sum p_den p_inv p_norm")
        self.pT_ps, self.pT, self.o_ps, self.oT, self.x1_ps, self.x1 = new("pT_ps pT o_ps oT x1_ps x1")
        self.h2T_ps, self.h2T, self.ck_ps, self.ck, self.cv_ps, self.cv = new("h2T_ps h2T ck_ps ck cv_ps cv")
        self.qp_ps, self.qp, self.sx_ps, self.sx, self.sx_max, self.sx_shift = new("qp_ps qp sx_ps sx sx_max sx_shift")
        self.px_exp, self.px_sum, self.px_inv, self.pxT_ps, self.pxT, self.avx_ps = new("px_exp px_sum px_inv pxT_ps pxT avx_ps")
        self.ox, self.oxT_ps, self.oxT, self.x2_ps, self.x2 = new("ox oxT_ps oxT x2_ps x2")
        self.h3T_ps, self.h3s, self.h3T, self.lg_ps, self.lg, self.top8 = new("h3T_ps h3s h3T lg_ps lg top8")
        self.topi, self.topd, self.top_exp, self.top_inv, self.top_w, self.onehot = new("topi topd top_exp top_inv top_w onehot")
        self.chosen, self.ohw, self.wd, self.hx_st = new("chosen ohw wd hx_st")
        self.rank_ps, self.rank, self.rank_used, self.slots, self.scat = new("rank_ps rank rank_used slots scat")
        self.sh_g, self.sh_u, self.sh_silu, self.sh_act, self.sh_y_ps, self.sh_y = new("sh_g sh_u sh_silu sh_act sh_y_ps sh_y")
        self.sh_st0, self.sh_st1, self.pad_st = new("sh_st0 sh_st1 pad_st")
        self.ix_ld, self.ix_f, self.ix_T, self.idx, self.cnt_f, self.cnt = new("ix_ld ix_f ix_T idx cnt_f cnt")


class ExpertSignals:
    def __init__(self, new):
        self.xT_ps, self.xT, self.gu_ps, self.act_s, self.act = new("xT_ps xT gu_ps act_s act")
        self.y_ps, self.y_w, self.scat_add, self.ix, self.wcol = new("y_ps y_w scat_add ix wcol")
        self.xh, self.wh, self.wl, self.eah, self.eal = new("xh wh wl eah eal")


class LateSignals:
    def __init__(self, new):
        self.w, self.idx, self.g, self.xT_ps, self.xT, self.gu_ps = new("w idx g xT_ps xT gu_ps")
        self.act_s, self.act, self.y_ps, self.y_w, self.add = new("act_s act y_ps y_w add")


class Stages:
    def __init__(self, A, Q, X, C):
        self.A, self.Q, self.X, self.C = A, Q, X, C


def build(nc, a, out):
    with ExitStack() as ctx:
        def sb(name, shape, dt=fp32):
            return ctx.enter_context(nc.sbuf_tensor(name, shape, dt))

        def semaphores(prefix):
            return lambda names: [ctx.enter_context(nc.semaphore(prefix + n)) for n in names.split()]

        s, m, o = Signals(semaphores("")), ExpertSignals(semaphores("m_")), LateSignals(semaphores("o_"))
        s.ring = [ctx.enter_context(nc.semaphore(f"ring{i}")) for i in range(RING)]
        s.gath = [ctx.enter_context(nc.semaphore(f"gath{i}")) for i in range(2)]

        w_all = sb("w_all", [P, 32 * 256 + 34 * 256])
        wc = w_all[:, 0:8192]
        w_up = w_all[:, 8192:10240]
        w_kv = w_all[:, 10240:11264]
        w_q = w_all[:, 11264:13312]
        w_kx = w_all[:, 13312:14336]
        w_out = w_all[:, 14336:16384]
        w_comp = w_all[:, 16384:16896]
        w_sg, w_su, w_sd = (w_all[:, 2048 * i:2048 * (i + 1)] for i in range(3))
        w_r = sb("w_r", [P, KC * NE])

        work = sb("work", [P, 4 * 1600 + 2048 + 1024 + 3 * 512])
        T16, Pm, PX, OT = (work[:, 1600 * i:1600 * (i + 1)] for i in range(4))
        qr = work[0:T, 6400:8448]
        rtmp = work[0:T, 8448:9472]
        h1, h2, xc = (work[0:T, 9472 + 512 * i:9984 + 512 * i] for i in range(3))
        h3x = sb("h3x", [T, HXW])
        h1T, h2T, h3s, qpT, ckT, oxT = (sb(n, [P, 400]) for n in ("h1T", "h2T", "h3s", "qpT", "ckT", "oxT"))
        hqT, kT, ctxT = (sb(n, [P, T]) for n in ("hqT", "kT", "ctxT"))
        kvs, vS, kr, ktmp = sb("kvs", [T, 2 * D]), sb("vS", [T, D]), sb("kr", [T, D]), sb("ktmp", [T, RD])
        junk = sb("junk", [T, D])
        ssq, qkv_var, rall, phalf = (sb(n, [T, NH + 1]) for n in ("ssq", "qkv_var", "rall", "phalf"))
        mx, sdiff, esink, den, rinv, mxx, denx, rx = (
            sb(n, [T, NH]) for n in ("mx", "sdiff", "esink", "den", "rinv", "mxx", "denx", "rx"))
        st = [sb(f"st{k}", [T, 6]) for k in range(3)]
        mv = [sb(f"mv{k}", [T, 2]) for k in range(3)]
        var = [sb(f"var{k}", [T, 2]) for k in range(3)]
        rstd = [sb(f"rstd{k}", [T, 2]) for k in range(3)]
        lgs, v8, i8, idxf = sb("lgs", [T, NE]), sb("v8", [T, 8]), sb("i8", [T, 8], u32), sb("idxf", [T, TOPK])
        d4, e4, sum4, inv4, w4 = (sb(n, [T, k]) for n, k in (("d4", 4), ("e4", 4), ("sum4", 1), ("inv4", 1), ("w4", 4)))
        oh, ohw, pick = sb("oh", [T, TOPK * NE]), sb("ohw", [T, TOPK * NE]), sb("pick", [T, TOPK * NE])
        chosen = sb("chosen", [T, NE], bf16)
        rk, run = sb("rk", [T, NE]), sb("run", [T, NE])
        slot, tok = sb("slot", [T, TOPK], i32), sb("tok", [T, 1], i32)
        ident, c64, s64 = sb("ident", [P, P]), sb("c64", [T, RD]), sb("s64", [T, RD])
        eid, runs, tokall = sb("eid", [T, TOPK * NE]), sb("runs", [T, NE]), sb("tokall", [T, NB], i32)
        identb, mask4 = sb("identb", [T, T], bf16), sb("mask4", [T, QW], bf16)
        tri, ones = sb("tri", [T, T], bf16), sb("ones", [T, T], bf16)
        wqk, wkn, sink = sb("wqk", [T, D]), sb("wkn", [T, D]), sb("sink", [T, NH])
        shtmp = ckT
        ytile = [sb(f"ytile{i}", [T, HID]) for i in range(2)]
        slots_w = [w_all[:, 6144 + WX * i:6144 + WX * (i + 1)] for i in range(3)] + [work[:, 0:WX]]
        w1s = [w[:, 0:2048] for w in slots_w]
        w2s = [w[:, 2048:3072] for w in slots_w]
        at = WX
        Xg = [[work[:, at + (2 * i + j) * HXW:at + (2 * i + j + 1) * HXW] for j in range(2)] for i in range(2)]
        at += 4 * HXW
        XT = [work[:, at + 1024 * i:at + 1024 * (i + 1)] for i in range(2)]
        at += 2048
        ea = work[:, at:at + 512]
        at += 512
        et = work[:, at:at + 512]
        at += 512
        Y = [work[:, at + 1024 * i:at + 1024 * (i + 1)] for i in range(2)]
        ixr, ixf = h1T[0:2 * NE, 0:P].bitcast(i32), h2T[0:2 * NE, 0:P]
        idx = sb("idx", [P, 2 * NE], i32)
        ixg, ixs = ([sb(f"{n}{i}", [P, FAST], i32) for i in range(2)] for n in ("ixg", "ixs"))
        wcol = [sb(f"wcol{i}", [P, FAST]) for i in range(RING)]
        cnt, most = sb("cnt", [1, NE], i32), sb("most", [1, 1], i32)
        oidx = kT[:, 0:1].bitcast(i32)

        with ExitStack() as early:
            def before(name, shape):
                return early.enter_context(nc.sbuf_tensor(name, shape, fp32))

            h3T = before("h3T", [P, KC * NTOK])
            resid = before("resid", [T, NB * HID])
            shact = before("shact", [P, 4 * QW])
            cv, ox, normw = (before(n, [T, HID]) for n in ("cv", "ox", "normw"))
        wh, wl = zip(*[(sb(f"wh{i}", [P, WX], f32r), sb(f"wl{i}", [P, WX], f32r)) for i in range(2)])
        xh, xl = zip(*[(sb(f"xh{i}", [P, KC * PADS], f32r), sb(f"xl{i}", [P, KC * PADS], f32r)) for i in range(2)])
        eh, el = sb("eh", [P, 2 * PADS], f32r), sb("el", [P, 2 * PADS], f32r)

        QS = ctx.enter_context(nc.psum_tensor("QS", [P, 2048], fp32))
        W = ctx.enter_context(nc.psum_tensor("W", [P, 2048], fp32))
        qb = [QS[:, 512 * i:512 * (i + 1)] for i in range(4)]
        wb = [W[:, 512 * i:512 * (i + 1)] for i in range(4)]

        hx = nc.dram_tensor("hx_rows", [ROWS, HXW], fp32, kind="Internal").ap()
        table = nc.dram_tensor("expert_lists", [NE * CAP, 1], i32, kind="Internal").ap()

        half = [[h3T[:, 0:2048], h3T[:, 2048:4096]], [work[:, 0:2048], work[:, 2048:4096]]]
        block = ctx.enter_context(nc.Block())

        def wait_alone(eng, sem, value):
            eng.wait_ge(sem, value)
            eng.sem_inc(s.passed, 1)

        def stages(b):
            if isinstance(b, int):
                return Stages(A=b < NB, Q=b + 1 < NB, X=1 <= b <= NB, C=b >= 2)
            return Stages(A=True, Q=True, X=True, C=True)

        def pipeline(eng, step):
            step(0)
            step(1)
            with eng.Fori(2, NB - 1) as b:
                step(b)
            for b in range(NB - 1, NB + 2):
                step(b)

        @block.sync
        def _(sp):
            xv = a["x"].rearrange("b t d -> t b d")
            rv = resid[:, :].rearrange("t (b d) -> t b d", d=HID)
            consts = [(ident, "c_ident"), (c64, "c_cos"), (s64, "c_sin"), (eid, "c_eid"), (runs, "c_runs"),
                      (tokall, "c_tok"), (identb, "c_identb"), (mask4, "c_mask"), (tri, "c_tri"), (ones, "c_ones"),
                      (wqk, "qn"), (wkn, "kn"), (sink, "sink"), (normw, "normw")]
            for g in range(G):
                if g >= 2:
                    sp.wait_ge(s.wc_ps, 4 * (g - 1))
                h, done = half[g % 2], (s.ld_half0, s.ld_half1)[g % 2]
                sp.dma_start(h[0].rearrange("p (k n) -> p k n", k=4),
                             a["w1T"][g].rearrange("(k p) n -> p k n", p=P)).then_inc(done, 16)
                sp.dma_start(h[1].rearrange("p (k n) -> p k n", k=4),
                             a["out_w2"][GI * g:GI * (g + 1), :].rearrange("(k p) n -> p k n", p=P)).then_inc(done, 16)
                if g == 0:
                    sp.dma_start(rv[:, 0:1, :], xv[:, 0:1, :]).then_inc(s.ld_x0, 16)
                    for t, n in consts:
                        sp.dma_start(t[:, :], a[n]).then_inc(s.ld_const, 16)
                if g == 1:
                    for t, n, k in ((w_comp, "wq_comp", KC), (w_up, "wq_up", 1), (w_kv, "wkv", KC)):
                        sp.dma_start(t.rearrange("p (k n) -> p k n", k=k),
                                     a[n].rearrange("(k p) n -> p k n", p=P)).then_inc(s.ld_w, 16)
                if g == 2:
                    sp.dma_start(rv[:, 1:NB, :], xv[:, 1:NB, :]).then_inc(s.ld_x, 16)
            for t, n, k in ((w_q, "WqT", KC), (w_kx, "WkvT", 1), (w_out, "WoutT", KC), (w_r, "routerT", KC)):
                sp.dma_start(t.rearrange("p (k n) -> p k n", k=k) if n != "routerT" else
                             t[:, :].rearrange("p (k n) -> p k n", k=k),
                             a[n].rearrange("(k p) n -> p k n", p=P)).then_inc(s.ld_wx, 16)
            sp.dma_start(table, a["c_table"]).then_inc(s.pad_st, 16)
            sp.dma_start(hx[NTOK:ROWS, :], a["c_zero"]).then_inc(s.pad_st, 16)
            sp.dma_start(out[NTOK:ROWS, :], a["c_zero"][:, 0:HID]).then_inc(s.pad_st, 16)

            def step(b):
                do = stages(b)
                if do.A:
                    src = a["ctxT"][bass.ds(b, 1), :, 0:T].rearrange("b k t -> (b k) t")
                    sp.wait_ge(s.cv_ps, b)
                    sp.dma_start(ctxT[:, :], src).then_inc(s.ld_ctx, 16)
                if isinstance(b, int) and b == NB:
                    sp.wait_ge(s.x1_ps, NB)
                    for t, n in ((w_sg, "sg"), (w_su, "su"), (w_sd, "sd")):
                        sp.dma_start(t.rearrange("p (k n) -> p k n", k=KC),
                                     a[n].rearrange("(k p) n -> p k n", p=P)).then_inc(s.ld_sh, 16)
                if do.C:
                    dst = hx[bass.ds(sp.snap(T * (b - 2)) if not isinstance(b, int) else T * (b - 2), T), :]
                    sp.wait_ge(s.wd, b - 1)
                    sp.dma_start(dst, h3x[:, :]).then_inc(s.hx_st, 16)

            pipeline(sp, step)

            sp.wait_ge(s.x2_ps, NB)

            def load_expert(e, u):
                src1 = a["w1"][bass.ds(e, 1), :, :].rearrange("e (k p) n -> p (e k) n", p=P)
                src2 = a["w2"][bass.ds(e, 1), :, :].rearrange("e (k p) n -> p (e k) n", p=P)
                return ((w1s[u].rearrange("p (k n) -> p k n", k=KC), src1),
                        (w2s[u].rearrange("p (k n) -> p k n", k=FE // P), src2))

            for u in range(RING):
                for dst, src in load_expert(u, u):
                    sp.dma_start(dst, src).then_inc(s.ring[u], 16)
            with sp.Fori(1, NE // RING) as r:
                e = r * RING
                for u in range(RING):
                    pair = load_expert(e + u, u)
                    sp.wait_ge(m.wl, 2 * (e + u - RING) + 2)
                    for dst, src in pair:
                        sp.dma_start(dst, src).then_inc(s.ring[u], 16)

            done = sp.alloc_register("sp_late")
            sp.reg_mov(done, 0)
            sp.wait_ge(s.cnt, 2)
            longest = sp.value_load(most[0:1, 0:1], min_val=0, max_val=NTOK)
            with sp.If(longest > BLK * FAST):
                with sp.Fori(0, NE) as e:
                    c = sp.value_load(cnt[0:1, bass.ds(e, 1)], min_val=0, max_val=NTOK)
                    with sp.If(c > BLK * FAST):
                        with sp.Fori(FAST, NBLK) as j:
                            with sp.If(c > BLK * j):
                                k = sp.snap(done)
                                pair = load_expert(e, 0)
                                isrc = table[bass.ds(CAP * e + BLK * j, BLK), :]
                                sp.wait_ge(m.y_ps, NE)
                                sp.wait_ge(o.add, 16 * k)
                                for dst, src in pair:
                                    sp.dma_start(dst, src).then_inc(o.w, 16)
                                sp.dma_start(oidx, isrc).then_inc(o.idx, 16)
                                sp.reg_add(done, done, 1)
                                sp.nop(nofuse=True)
                        sp.nop(nofuse=True)
                sp.nop(nofuse=True)

        @block.tensor
        def _(pe):
            mm, tr = nc.tensor.matmul, nc.tensor.transpose
            def join(g):
                pe.wait_ge((s.ld_half0, s.ld_half1)[g % 2], 32 * (g // 2 + 1))
                for i in range(4):
                    n = 4 * g + i
                    if n >= 4:
                        pe.wait_ge(s.wc, n - 3)
                    if n == 14:
                        pe.wait_ge(s.kv, 1)
                    for k in range(4):
                        w1, w2 = half[g % 2]
                        last = mm(wb[n % 4], w1[:, 512 * k + P * i:512 * k + P * (i + 1)],
                                  w2[:, 512 * k:512 * (k + 1)], start=k == 0, stop=k == 3)
                    last.then_inc(s.wc_ps, 1)

            def to_columns(dst, src, n=KC, w=P):
                for k in range(n):
                    last = tr(dst[0:w, T * k:T * (k + 1)], src[0:T, w * k:w * (k + 1)], ident[0:T, 0:T])
                return last

            def ln1_columns(c):
                pe.wait_ge(s.ln1_h, c + 1)
                to_columns(wb[0], h1).then_inc(s.h1T_ps, 1)

            def compress(c):
                pe.wait_ge(s.h1T, c + 1)
                for k in range(KC):
                    last = mm(wb[1][:, 0:T], w_comp[:, P * k:P * (k + 1)], h1T[:, T * k:T * (k + 1)],
                              start=k == 0, stop=k == KC - 1)
                last.then_inc(s.hq_ps, 1)
                for k in range(KC):
                    last = mm(wb[2][0:T, 0:2 * D], h1T[:, T * k:T * (k + 1)], w_kv[:, 256 * k:256 * (k + 1)],
                              start=k == 0, stop=k == KC - 1)
                last.then_inc(s.kv_ps, 1)

            def queries(c):
                pe.wait_ge(s.hqT, c + 1)
                for i in range(4):
                    last = mm(qb[i][0:T, :], hqT[:, :], w_up[:, 512 * i:512 * (i + 1)], start=True, stop=True)
                last.then_inc(s.q_ps, 1)

            def project(b, heads):
                for h in heads:
                    if h % QH == 0:
                        pe.wait_ge(s.oT, 4 * b + h // QH + 1)
                    last = mm(wb[0][0:T, :], OT[:, T * h:T * (h + 1)], wc[:, 512 * h:512 * (h + 1)],
                              start=h == 0, stop=h == NH - 1)
                return last

            def step(b):
                do = stages(b)
                if do.A:
                    pe.wait_ge(s.k_scaled, b + 1)
                    pe.wait_ge(s.q_rot, b + 1)
                    if do.C:
                        pe.wait_ge(s.pxT, 4 * (b - 1))
                    tr(qb[0][:, 0:T], kr[:, :], ident[0:T, 0:T]).then_inc(s.kT_ps, 1)
                    for i in range(4):
                        if i == 0 and do.X:
                            pe.wait_ge(s.x1, b)
                        if i == 1 and do.C:
                            pe.wait_ge(s.rank_used, b - 2)
                        if i == 3 and do.C:
                            pe.wait_ge(s.x2, b - 1)
                        for j in range(QH):
                            h = QH * i + j
                            last = tr(wb[i][:, T * j:T * (j + 1)], qr[:, D * h:D * (h + 1)], ident[0:T, 0:T])
                        last.then_inc(s.qT_ps, 1)
                    pe.wait_ge(s.kT, b + 1)
                    for i in range(4):
                        pe.wait_ge(s.qT, 4 * b + i + 1)
                        mm(qb[i][0:T, 0:QW], identb[:, :], mask4[:, :], start=True, stop=False)
                        for j in range(QH):
                            h = QH * i + j
                            last = mm(qb[i][0:T, T * j:T * (j + 1)], T16[:, T * h:T * (h + 1)], kT[:, :],
                                      start=False, stop=j == QH - 1)
                        last.then_inc(s.s_ps, 1)
                if do.X:
                    pe.wait_ge(s.ln2_h, b)
                    to_columns(wb[0], h2).then_inc(s.h2T_ps, 1)
                    pe.wait_ge(s.ld_ctx, 16 * b)
                    for i in range(4):
                        last = mm(wb[2][:, T * i:T * (i + 1)], w_kx[:, P * i:P * (i + 1)], ctxT[:, :],
                                  start=i == 0, stop=True, skip_group_check=True)
                    last.then_inc(s.ck_ps, 1)
                    if do.C:
                        pe.wait_ge(s.x2, b - 1)
                    mm(wb[3][0:T, :], ctxT[:, :], w_kx[:, 512:1024], start=True, stop=True).then_inc(s.cv_ps, 1)
                    pe.wait_ge(s.h2T, b)
                    if do.C:
                        pe.wait_ge(s.rank_used, b - 2)
                    for i in range(4):
                        for k in range(KC):
                            last = mm(wb[1][:, T * i:T * (i + 1)], w_q[:, 512 * k + P * i:512 * k + P * (i + 1)],
                                      h2T[:, T * k:T * (k + 1)], start=k == 0, stop=k == KC - 1)
                    last.then_inc(s.qp_ps, 1)
                if do.Q:
                    ln1_columns(b + 1)
                if do.X:
                    pe.wait_ge(s.s_scaled, 4 * (b + 1) if do.A else 4 * NB)
                    if do.C:
                        pe.wait_ge(s.pxT, 4 * (b - 1))
                    pe.wait_ge(s.ck, b)
                    for j in range(4):
                        mm(qb[j][0:T, 0:QW], identb[:, :], mask4[:, :], start=True, stop=False)
                    pe.wait_ge(s.qp, b)
                    for i in range(4):
                        for j in range(4):
                            r = slice(DX * j, DX * (j + 1))
                            last = mm(qb[j][0:T, T * i:T * (i + 1)], qpT[r, T * i:T * (i + 1)],
                                      ckT[r, T * i:T * (i + 1)], start=False, stop=i == 3)
                    last.then_inc(s.sx_ps, 1)
                if do.Q:
                    compress(b + 1)
                    pe.wait_ge(s.s_scaled, 4 * b + 4)
                    if do.X:
                        pe.wait_ge(s.sx, b)
                    queries(b + 1)
                if do.A:
                    pe.wait_ge(s.p_norm, b + 1)
                    for i in range(4):
                        if i == 2 and do.Q:
                            pe.wait_ge(s.kv, b + 2)
                        if i == 3 and do.X:
                            pe.wait_ge(s.cv, b)
                        for j in range(QH):
                            h = QH * i + j
                            last = tr(wb[i][0:T, T * j:T * (j + 1)], Pm[0:T, T * h:T * (h + 1)], ident[0:T, 0:T])
                        last.then_inc(s.pT_ps, 1)
                    pe.wait_ge(s.v, b + 1)
                    for i in range(4):
                        pe.wait_ge(s.pT, 4 * b + i + 1)
                        mm(wb[i][:, 0:QW], vS[:, :], T16[0:T, QW * i:QW * (i + 1)], start=True, stop=True)\
                            .then_inc(s.o_ps, 1)
                if do.C:
                    if do.A:
                        pe.wait_ge(s.oT, 4 * b + 2)
                    pe.wait_ge(s.rank_used, b - 2)
                    pe.wait_ge(s.ln3_h, b - 1)
                    to_columns(wb[1], h3x).then_inc(s.h3T_ps, 1)
                if do.A:
                    project(b, range(0, 12))
                if do.C:
                    pe.wait_ge(s.h3s, b - 1)
                    for k in range(KC):
                        last = mm(wb[2][0:T, 0:NE], h3s[:, T * k:T * (k + 1)], w_r[:, NE * k:NE * (k + 1)],
                                  start=k == 0, stop=k == KC - 1)
                    last.then_inc(s.lg_ps, 1)
                if do.X:
                    pe.wait_ge(s.px_exp, b)
                    if do.Q:
                        pe.wait_ge(s.q_out, b + 2)
                        pe.wait_ge(s.q_ssq, b + 2)
                    for i in range(4):
                        for j in range(QH):
                            h = QH * i + j
                            last = tr(qb[i][0:T, T * j:T * (j + 1)], PX[0:T, T * h:T * (h + 1)], ident[0:T, 0:T])
                        last.then_inc(s.pxT_ps, 1)
                if do.A:
                    project(b, range(12, 14))
                if do.X:
                    if do.C:
                        pe.wait_ge(s.h3T, b - 1)
                    pe.wait_ge(s.cv, b)
                    for j in range(4):
                        pe.wait_ge(s.pxT, 4 * (b - 1) + j + 1)
                        for i in range(4):
                            h = 4 * i + j
                            last = mm(wb[1][0:T, DX * h:DX * (h + 1)], T16[0:T, T * (4 * j + i):T * (4 * j + i + 1)],
                                      cv[:, DX * h:DX * (h + 1)], start=i == 0 and j == 0, stop=True,
                                      skip_group_check=True)
                    last.then_inc(s.avx_ps, 1)
                if do.A:
                    project(b, range(14, 16)).then_inc(s.x1_ps, 1)
                if do.X:
                    pe.wait_ge(s.ox, b)
                    if do.C:
                        pe.wait_ge(s.lg, b - 1)
                    to_columns(wb[2], ox).then_inc(s.oxT_ps, 1)
                if do.C:
                    pe.wait_ge(s.chosen, b - 1)
                    pe.wait_ge(s.h3T, b - 1)
                    mm(wb[1][0:T, 0:NE], tri[:, :], chosen[:, :], start=True, stop=True)
                    mm(wb[1][0:T, NE:2 * NE], ones[:, :], chosen[:, :], start=True, stop=True).then_inc(s.rank_ps, 1)
                if do.X:
                    pe.wait_ge(s.oxT, b)
                    for k in range(KC):
                        last = mm(wb[3][0:T, :], oxT[:, T * k:T * (k + 1)], w_out[:, 512 * k:512 * (k + 1)],
                                  start=k == 0, stop=k == KC - 1)
                    last.then_inc(s.x2_ps, 1)

            for g in range(G - 1):
                join(g)
            pe.wait_ge(s.ld_const, 16 * 14)
            pe.wait_ge(s.ld_w, 48)
            pe.wait_ge(s.wc, 4 * (G - 1))
            ln1_columns(0)
            compress(0)
            queries(0)
            join(G - 1)
            pe.wait_ge(s.wc, 4 * G)
            pe.wait_ge(s.ld_wx, 64)
            pe.wait_ge(s.h1T, 1)
            pipeline(pe, step)

            pe.wait_ge(s.ld_sh, 48)
            pe.wait_ge(s.x2, NB)
            pe.wait_ge(s.h3T, NB)
            pe.wait_ge(s.rank_used, NB)
            def shared_inner(g):
                for f in range(4):
                    pe.wait_ge(s.sh_act, 4 * g + f - 1) if f >= 2 else pe.wait_ge(s.sh_act, 4 * g)
                    for w, bank, done in ((w_sg, qb[f % 2], s.sh_g), (w_su, qb[2 + f % 2], s.sh_u)):
                        for k in range(KC):
                            last = mm(bank[:, 0:QW], w[:, 512 * k + P * f:512 * k + P * (f + 1)],
                                      h3T[:, bass.ds(g * QW + NTOK * k, QW)], start=k == 0, stop=k == KC - 1)
                        last.then_inc(done, 1)
                pe.wait_ge(s.sh_act, 4 * g + 4)

            def shared_outer(g):
                for t in range(4):
                    pe.wait_ge(s.sh_y, 4 * g)
                    for f in range(4):
                        last = mm(wb[t][0:T, :], shact[:, QW * f + T * t:QW * f + T * (t + 1)],
                                  w_sd[:, 512 * f:512 * (f + 1)], start=f == 0, stop=f == 3)
                    last.then_inc(s.sh_y_ps, 1)

            with pe.Fori(0, 3) as g:
                shared_inner(g)
                shared_outer(g)
            shared_inner(3)
            pe.wait_ge(s.ix_f, 1)
            tr(qb[0][:, 0:2 * NE], ixf, ident[0:2 * NE, 0:2 * NE]).then_inc(s.ix_T, 1)
            shared_outer(3)
            pe.wait_ge(s.idx, 1)

            def x_columns(e, u):
                pe.wait_ge(s.gath[u % 2], 16 * e + (32 if u % 2 == 0 else 16))
                pe.wait_ge(m.xT, e)
                for j in range(FAST):
                    for k in range(KC):
                        last = tr(QS[:, 256 * k + P * j:256 * k + P * (j + 1)], Xg[u % 2][j][:, P * k:P * (k + 1)], ident[:, :])
                last.then_inc(m.xT_ps, 1)

            def split_product(dst, ah, al, bh, bl, start, stop):
                mm(dst, ah, bh, start=start, stop=False)
                mm(dst, ah, bl, start=False, stop=False)
                return mm(dst, al, bh, start=False, stop=stop)

            def inner(e, u, v):
                pe.wait_ge(m.xT, e + 1)
                pe.wait_ge(m.wl, 2 * e + 1)
                if not isinstance(e, int) or e > 0:
                    pe.wait_ge(m.act, 2 * e - 1 + v)
                for i, f in enumerate((v, 2 + v)):
                    for k in range(KC):
                        w, x = slice(512 * k + P * f, 512 * k + P * (f + 1)), slice(256 * k, 256 * (k + 1))
                        last = split_product(QS[:, 1024 + 512 * v + 256 * i:1280 + 512 * v + 256 * i], wh[u % 2][:, w],
                                             wl[u % 2][:, w], xh[u % 2][:, x], xl[u % 2][:, x], k == 0, k == KC - 1)
                last.then_inc(m.gu_ps, 1)

            def outer(e, u):
                pe.wait_ge(m.eal, e + 1)
                pe.wait_ge(m.wl, 2 * e + 2)
                pe.wait_ge(m.y_w, e)
                for j in range(FAST):
                    for f in range(FE // P):
                        c, w = slice(256 * f + P * j, 256 * f + P * (j + 1)), slice(2048 + 512 * f, 2560 + 512 * f)
                        last = split_product(wb[j][:, :], eh[:, c], el[:, c], wh[u % 2][:, w], wl[u % 2][:, w],
                                             f == 0, f == FE // P - 1)
                last.then_inc(m.y_ps, 1)

            x_columns(0, 0)
            x_columns(1, 1)
            inner(0, 0, 0)
            inner(0, 0, 1)
            with pe.Fori(0, NE // 2 - 1) as r:
                for u in (1, 2):
                    e = r * 2 + u
                    x_columns(e + 1, u + 1)
                    inner(e, u, 0)
                    outer(e - 1, u - 1)
                    inner(e, u, 1)
            inner(NE - 1, NE - 1, 0)
            outer(NE - 2, NE - 2)
            inner(NE - 1, NE - 1, 1)
            outer(NE - 1, NE - 1)

            done = pe.alloc_register("pe_late")
            pe.reg_mov(done, 0)
            pe.wait_ge(s.cnt, 2)
            longest = pe.value_load(most[0:1, 0:1], min_val=0, max_val=NTOK)
            with pe.If(longest > BLK * FAST):
                with pe.Fori(0, NE) as e:
                    c = pe.value_load(cnt[0:1, bass.ds(e, 1)], min_val=0, max_val=NTOK)
                    with pe.If(c > BLK * FAST):
                        with pe.Fori(FAST, NBLK) as j:
                            with pe.If(c > BLK * j):
                                n = pe.snap(done)
                                pe.wait_ge(m.y_w, NE)
                                pe.wait_ge(o.y_w, n)
                                pe.wait_ge(o.g, 16 * n + 16)
                                for k in range(KC):
                                    last = tr(QS[:, P * k:P * (k + 1)], Xg[0][0][:, P * k:P * (k + 1)], ident[:, :])
                                last.then_inc(o.xT_ps, 1)
                                pe.wait_ge(o.xT, n + 1)
                                pe.wait_ge(o.w, 32 * n + 32)
                                for f in range(4):
                                    for k in range(KC):
                                        last = mm(QS[:, 1024 + P * f:1024 + P * (f + 1)], w1s[0][:, 512 * k + P * f:512 * k + P * (f + 1)],
                                                  XT[0][:, P * k:P * (k + 1)], start=k == 0, stop=k == KC - 1)
                                last.then_inc(o.gu_ps, 1)
                                pe.wait_ge(o.act, n + 1)
                                for f in range(FE // P):
                                    last = mm(wb[0][:, :], ea[:, P * f:P * (f + 1)], w2s[0][:, 512 * f:512 * (f + 1)],
                                              start=f == 0, stop=f == FE // P - 1)
                                last.then_inc(o.y_ps, 1)
                                pe.reg_add(done, done, 1)
                                pe.nop(nofuse=True)
                        pe.nop(nofuse=True)
                pe.nop(nofuse=True)

        @block.scalar
        def _(act):
            fn = nc.scalar.activation

            def copy(dst, src):
                return fn(dst, src, ACT.Copy)

            def joined(heads):
                for n in heads:
                    act.wait_ge(s.wc_ps, n + 1)
                    act.wait_ge(s.wc, n)
                    copy(wc[:, 512 * n:512 * (n + 1)], wb[n % 4]).then_inc(s.wc, 1)

            def ln1_columns(c):
                act.wait_ge(s.h1T_ps, c + 1)
                act.wait_ge(s.kv_ps, c)
                copy(h1T[:, :], wb[0][:, 0:QW]).then_inc(s.h1T, 1)

            def compressed(c):
                act.wait_ge(s.hq_ps, c + 1)
                act.wait_ge(s.q_ps, c)
                copy(hqT[:, :], wb[1][:, 0:T]).then_inc(s.hqT, 1)
                act.wait_ge(s.kv_ps, c + 1)
                act.wait_ge(s.v, c)
                act.wait_ge(s.k_rot, c)
                copy(kvs[:, :], wb[2][0:T, 0:2 * D]).then_inc(s.kv, 1)

            def queries_out(c):
                act.wait_ge(s.q_ps, c + 1)
                act.wait_ge(s.qT_ps, 4 * c)
                copy(qr, QS[0:T, :]).then_inc(s.q_out, 1)

            def squares(c):
                act.wait_ge(s.q_rot, c + 1)
                act.wait_ge(s.k_rot, c + 1)
                act.wait_ge(s.qk_var, c)
                fn(junk[:, :], kr[:, :], ACT.Square, accum_out=ssq[:, NH:NH + 1])
                for h in range(NH):
                    last = fn(QS[0:T, D * h:D * (h + 1)], qr[:, D * h:D * (h + 1)], ACT.Square, accum_out=ssq[:, h:h + 1])
                last.then_inc(s.q_ssq, 1)

            def step(b):
                do = stages(b)
                if do.A:
                    act.wait_ge(s.kT_ps, b + 1)
                    act.wait_ge(s.s_ps, 4 * b)
                    copy(kT[:, :], qb[0][:, 0:T]).then_inc(s.kT, 1)
                    act.wait_ge(s.kv, b + 1)
                    act.wait_ge(s.o_ps, 4 * b)
                    copy(vS[:, :], kvs[:, D:2 * D]).then_inc(s.v, 1)
                    if do.C:
                        act.wait_ge(s.avx_ps, b - 1)
                    for i in range(4):
                        act.wait_ge(s.qT_ps, 4 * b + i + 1)
                        copy(T16[:, QW * i:QW * (i + 1)], wb[i][:, 0:QW]).then_inc(s.qT, 1)
                if do.X:
                    act.wait_ge(s.h2T_ps, b)
                    act.wait_ge(s.qp_ps, b - 1)
                    copy(h2T[:, :], wb[0][:, 0:QW]).then_inc(s.h2T, 1)
                    act.wait_ge(s.ck_ps, b)
                    act.wait_ge(s.sx_ps, b - 1)
                    copy(ckT[:, :], wb[2][:, 0:QW]).then_inc(s.ck, 1)
                    act.wait_ge(s.cv_ps, b)
                    act.wait_ge(s.avx_ps, b - 1)
                    copy(cv[:, :], wb[3][0:T, :]).then_inc(s.cv, 1)
                    act.wait_ge(s.qp_ps, b)
                    copy(qpT[:, :], wb[1][:, 0:QW]).then_inc(s.qp, 1)
                if do.Q:
                    ln1_columns(b + 1)
                if do.A:
                    act.wait_ge(s.s_shift, b + 1)
                    fn(Pm[0:T, :], Pm[0:T, :], ACT.Exp).then_inc(s.p_exp, 1)
                    act.wait_ge(s.s_sink, b + 1)
                    act.wait_ge(s.p_den, b)
                    fn(esink[:, :], sdiff[:, :], ACT.Exp).then_inc(s.e_sink, 1)
                if do.X:
                    act.wait_ge(s.sx_ps, b)
                    act.wait_ge(s.pxT_ps, 4 * (b - 1))
                    fn(PX[0:T, :].rearrange("t (a n) -> t a n", a=4),
                       QS[0:T, :].rearrange("t (a n) -> t a n", a=4)[:, :, 0:QW], ACT.Copy,
                       scale=DX ** -0.5).then_inc(s.sx, 1)
                if do.Q:
                    compressed(b + 1)
                    queries_out(b + 1)
                if do.A:
                    act.wait_ge(s.s_ps, 4 * b + 4)
                    for i in range(4):
                        act.wait_ge(s.pT_ps, 4 * b + i + 1)
                        copy(T16[0:T, QW * i:QW * (i + 1)], wb[i][0:T, 0:QW]).then_inc(s.pT, 1)
                    act.wait_ge(s.x1_ps, b)
                    for i in range(4):
                        act.wait_ge(s.o_ps, 4 * b + i + 1)
                        copy(OT[:, QW * i:QW * (i + 1)], wb[i][:, 0:QW]).then_inc(s.oT, 1)
                if do.C:
                    act.wait_ge(s.h3T_ps, b - 1)
                    act.wait_ge(s.lg_ps, b - 2)
                    copy(h3s[:, :], wb[1][:, 0:QW]).then_inc(s.h3s, 1)
                    copy(h3T[:, :].rearrange("p (k n) -> p k n", k=KC)[:, :, bass.ds(T * (b - 2), T)],
                         wb[1][:, 0:QW].rearrange("p (k n) -> p k n", k=KC)).then_inc(s.h3T, 1)
                if do.X:
                    act.wait_ge(s.sx_shift, b)
                    fn(PX[0:T, :], PX[0:T, :], ACT.Exp).then_inc(s.px_exp, 1)
                if do.Q:
                    squares(b + 1)
                if do.C:
                    act.wait_ge(s.topd, b - 1)
                    act.wait_ge(s.top_w, b - 2)
                    fn(e4[:, :], d4[:, :], ACT.Exp, accum_out=sum4[:, :]).then_inc(s.top_exp, 1)
                if do.X:
                    if do.A:
                        act.wait_ge(s.o_ps, 4 * b + 4)
                    else:
                        act.wait_ge(s.avx_ps, b - 1)
                    for i in range(4):
                        act.wait_ge(s.pxT_ps, 4 * (b - 1) + i + 1)
                        copy(T16[0:T, QW * i:QW * (i + 1)], qb[i][0:T, 0:QW]).then_inc(s.pxT, 1)
                    act.wait_ge(s.oxT_ps, b)
                    act.wait_ge(s.x2_ps, b - 1)
                    copy(oxT[:, :], wb[2][:, 0:QW]).then_inc(s.oxT, 1)

            joined(range(0, 12, 2))
            ln1_columns(0)
            compressed(0)
            queries_out(0)
            joined(range(12, 16, 2))
            squares(0)
            pipeline(act, step)

            with act.Fori(0, 4) as g:
                for f in range(4):
                    act.wait_ge(s.sh_g, 4 * g + f + 1)
                    act.wait_ge(s.sh_act, 4 * g + f)
                    fn(shtmp[:, :], qb[f % 2][:, 0:QW], ACT.Silu).then_inc(s.sh_silu, 1)

            def weights_high(e, u, part, done):
                c = (slice(0, 2048), slice(2048, WX))[part]
                copy(wh[u % 2][:, c], slots_w[u % RING][:, c]).then_inc(done, 1)

            def rows_high(e, u):
                act.wait_ge(m.xT_ps, e + 1)
                copy(xh[u % 2][:, :], QS[:, 0:1024]).then_inc(m.xh, 1)

            def weigh(e, u):
                act.wait_ge(m.y_ps, e + 1)
                act.wait_ge(m.wcol, FAST * (e + 1))
                if not isinstance(e, int):
                    act.wait_ge(m.scat_add, 32 * (e - (0 if u == 0 else 1)))
                elif e >= 2:
                    act.wait_ge(m.scat_add, 32 * (e - 1))
                for j in range(FAST):
                    last = fn(Y[u % 2][:, 512 * j:512 * (j + 1)], wb[j][:, :], ACT.Copy, scale=wcol[u % RING][:, j:j + 1])
                last.then_inc(m.y_w, 1)

            def expert(e, u):
                more = not isinstance(e, int) or e + 1 < NE
                if more:
                    rows_high(e + 1, u + 1)
                    act.wait_ge(s.ring[(u + 1) % RING], ring_loads(e, u))
                    weights_high(e + 1, u + 1, 0, m.wh)
                act.wait_ge(m.gu_ps, 2 * e + 1)
                act.wait_ge(m.act, 2 * e)
                fn(et[:, 0:256], QS[:, 1024:1280], ACT.Silu).then_inc(m.act_s, 1)
                if not isinstance(e, int) or e > 0:
                    weigh(e - 1, u - 1)
                act.wait_ge(m.gu_ps, 2 * e + 2)
                fn(et[:, 256:512], QS[:, 1536:1792], ACT.Silu).then_inc(m.act_s, 1)
                act.wait_ge(m.act, 2 * e + 2)
                act.wait_ge(m.y_ps, e)
                copy(eh[:, :], ea).then_inc(m.eah, 1)
                if more:
                    weights_high(e + 1, u + 1, 1, m.wh)

            def ring_loads(e, u):
                return 32 * ((e + 1) // RING + 1) if isinstance(e, int) else 8 * (e - u) + 32 * ((u + 1) // RING + 1)

            act.wait_ge(s.sh_u, 16)
            act.wait_ge(s.ring[0], 32)
            weights_high(0, 0, 0, m.wh)
            weights_high(0, 0, 1, m.wh)
            act.wait_ge(s.sh_y, NB)
            rows_high(0, 0)
            expert(0, 0)
            with act.Fori(0, NE // RING - 1) as r:
                for u in range(1, RING + 1):
                    expert(r * RING + u, u)
            for e in range(NE - 3, NE):
                expert(e, e)
            weigh(NE - 1, NE - 1)

            done = act.alloc_register("act_late")
            act.reg_mov(done, 0)
            act.wait_ge(s.cnt, 2)
            longest = act.value_load(most[0:1, 0:1], min_val=0, max_val=NTOK)
            with act.If(longest > BLK * FAST):
                with act.Fori(0, NE) as e:
                    c = act.value_load(cnt[0:1, bass.ds(e, 1)], min_val=0, max_val=NTOK)
                    with act.If(c > BLK * FAST):
                        with act.Fori(FAST, NBLK) as j:
                            with act.If(c > BLK * j):
                                n = act.snap(done)
                                act.wait_ge(o.gu_ps, n + 1)
                                fn(et[:, 0:256], QS[:, 1024:1280], ACT.Silu).then_inc(o.act_s, 1)
                                act.wait_ge(o.y_ps, n + 1)
                                act.wait_ge(m.scat_add, 32 * NE)
                                act.wait_ge(o.add, 16 * n)
                                fn(Y[0][:, 0:512], wb[0][:, :], ACT.Copy, scale=Xg[0][0][:, bass.ds(HID + e, 1)]).then_inc(o.y_w, 1)
                                act.reg_add(done, done, 1)
                                act.nop(nofuse=True)
                        act.nop(nofuse=True)
                act.nop(nofuse=True)

        @block.vector
        def _(dve):
            tt, ts, red = nc.vector.tensor_tensor, nc.vector.tensor_scalar, nc.vector.tensor_reduce

            def per_head(v, n, w=T):
                return v.unsqueeze(2).to_broadcast([T, n, w])

            nc.vector.memset(phalf[:, :], -0.5).then_inc(s.wqk, 1)
            dve.wait_ge(s.ld_const, 16 * 14)
            nc.vector.scalar_tensor_tensor(out=wqk[:, :], in0=wqk[:, :], scalar=math.sqrt(D), in1=wkn[:, :],
                                           op0=ALU.mult, op1=ALU.mult).then_inc(s.wqk, 1)
            nc.vector.tensor_copy(run[:, :], runs[:, :]).then_inc(s.wqk, 1)
            dve.wait_ge(s.wqk, 3)
            def joined(heads):
                for n in heads:
                    dve.wait_ge(s.wc_ps, n + 1)
                    dve.wait_ge(s.wc, n)
                    nc.vector.tensor_copy(wc[:, 512 * n:512 * (n + 1)], wb[n % 4]).then_inc(s.wc, 1)

            def row(c):
                return resid[:, bass.ds(HID * c, HID)]

            def ln_stats(k, c, stats, done):
                nc.vector.bn_stats(st[k][:, :], row(c)).then_inc(stats, 1)
                wait_alone(dve, stats, 2 * c + 1)
                nc.vector.bn_aggr(mv[k][:, :], st[k][:, :]).then_inc(stats, 1)
                dve.wait_ge(stats, 2 * c + 2)
                ts(var[k][:, 0:1], mv[k][:, 1:2], 1e-5, None, ALU.add).then_inc(done, 1)

            def ln1_apply(c):
                dve.wait_ge(s.ln1_rstd, c + 1)
                dve.wait_ge(s.h1T_ps, c)
                ts(h1, row(c), mv[0][:, 0:1], rstd[0][:, 0:1], ALU.subtract, ALU.mult).then_inc(s.ln1_h, 1)

            def rotate(c):
                r3 = qr.rearrange("t (h d) -> t h d", d=D)
                t3 = rtmp.rearrange("t (h d) -> t h d", d=RD)
                hr = RD // 2
                dve.wait_ge(s.kv, c + 1)
                dve.wait_ge(s.kT_ps, c)
                tt(kr[:, 0:RD], kvs[:, 0:RD], c64[:, :], ALU.mult).then_inc(s.k_parts, 1)
                tt(ktmp[:, 0:hr], kvs[:, hr:RD], s64[:, 0:hr], ALU.mult).then_inc(s.k_parts, 1)
                tt(ktmp[:, hr:RD], kvs[:, 0:hr], s64[:, hr:RD], ALU.mult).then_inc(s.k_parts, 1)
                nc.vector.tensor_copy(kr[:, RD:D], kvs[:, RD:D])
                dve.wait_ge(s.k_parts, 3 * c + 3)
                tt(kr[:, 0:RD], kr[:, 0:RD], ktmp[:, :], ALU.add).then_inc(s.k_rot, 1)
                dve.wait_ge(s.q_out, c + 1)
                tt(t3[:, :, 0:hr], r3[:, :, hr:RD], s64[:, 0:hr].unsqueeze(1).to_broadcast([T, NH, hr]), ALU.mult)\
                    .then_inc(s.q_parts, 1)
                tt(t3[:, :, hr:RD], r3[:, :, 0:hr], s64[:, hr:RD].unsqueeze(1).to_broadcast([T, NH, hr]), ALU.mult)\
                    .then_inc(s.q_parts, 1)
                dve.wait_ge(s.q_parts, 3 * c + 2)
                tt(r3[:, :, 0:RD], r3[:, :, 0:RD], c64[:, :].unsqueeze(1).to_broadcast([T, NH, RD]), ALU.mult)\
                    .then_inc(s.q_parts, 1)
                dve.wait_ge(s.q_parts, 3 * c + 3)
                tt(r3[:, :, 0:RD], r3[:, :, 0:RD], t3, ALU.add).then_inc(s.q_rot, 1)

            def norms(c):
                dve.wait_ge(s.q_ssq, c + 1)
                dve.wait_ge(s.qk_rstd, c)
                ts(qkv_var[:, :], ssq[:, :], D * 1e-6, None, ALU.add).then_inc(s.qk_var, 1)

            def scale_keys(c):
                dve.wait_ge(s.k_rot, c + 1)
                dve.wait_ge(s.qk_rstd, c + 1)
                nc.vector.scalar_tensor_tensor(out=kr[:, :], in0=kr[:, :], scalar=rall[:, NH:NH + 1], in1=wqk[:, :],
                                               op0=ALU.mult, op1=ALU.mult).then_inc(s.k_scaled, 1)

            def step(b):
                do = stages(b)
                if do.Q:
                    if isinstance(b, int) and b == 0:
                        dve.wait_ge(s.ld_x, 16)
                    ln_stats(0, b + 1, s.ln1_stats, s.ln1_var)
                if do.A:
                    dve.wait_ge(s.qk_rstd, b + 1)
                    dve.wait_ge(s.pT_ps, 4 * b)
                    for i in range(4):
                        dve.wait_ge(s.s_ps, 4 * b + i + 1)
                        tt(Pm[0:T, QW * i:QW * (i + 1)].rearrange("t (h n) -> t h n", n=T),
                           qb[i][0:T, 0:QW].rearrange("t (h n) -> t h n", n=T),
                           per_head(rall[:, QH * i:QH * (i + 1)], QH), ALU.mult).then_inc(s.s_scaled, 1)
                P3 = Pm[0:T, :].rearrange("t (h n) -> t h n", n=T)
                X3 = PX[0:T, :].rearrange("t (h n) -> t h n", n=T)
                if do.A:
                    dve.wait_ge(s.s_scaled, 4 * b + 4)
                    red(mx[:, :], P3, AX.X, ALU.max).then_inc(s.s_max, 1)
                    dve.wait_ge(s.s_max, 2 * b + 1)
                    tt(mx[:, :], mx[:, :], sink[:, :], ALU.max).then_inc(s.s_max, 1)
                if do.Q:
                    ln1_apply(b + 1)
                if do.A:
                    dve.wait_ge(s.s_max, 2 * b + 2)
                    tt(P3, P3, per_head(mx[:, :], NH), ALU.subtract).then_inc(s.s_shift, 1)
                    tt(sdiff[:, :], sink[:, :], mx[:, :], ALU.subtract).then_inc(s.s_sink, 1)
                if do.C:
                    c = b - 2
                    dve.wait_ge(s.ln3_rstd, c + 1)
                    ts(xc, row(c), mv[2][:, 0:1], None, ALU.subtract).then_inc(s.ln3_xc, 1)
                    dve.wait_ge(s.ln3_xc, c + 1)
                    dve.wait_ge(s.h3T_ps, c)
                    dve.wait_ge(s.hx_st, 16 * c)
                    nc.vector.scalar_tensor_tensor(out=h3x[:, 0:HID], in0=xc, scalar=rstd[2][:, 1:2], in1=normw[:, :],
                                                   op0=ALU.mult, op1=ALU.mult).then_inc(s.ln3_h, 1)
                    nc.vector.scalar_tensor_tensor(out=row(c), in0=xc, scalar=rstd[2][:, 0:1], in1=row(c),
                                                   op0=ALU.mult, op1=ALU.add).then_inc(s.ln3_base, 1)
                if do.A:
                    dve.wait_ge(s.p_exp, b + 1)
                    red(den[:, :], P3, AX.X, ALU.add).then_inc(s.p_sum, 1)
                    dve.wait_ge(s.p_sum, b + 1)
                    dve.wait_ge(s.e_sink, b + 1)
                    tt(den[:, :], den[:, :], esink[:, :], ALU.add).then_inc(s.p_den, 1)
                    dve.wait_ge(s.p_den, b + 1)
                    nc.vector.reciprocal(rinv[:, :], den[:, :]).then_inc(s.p_inv, 1)
                    dve.wait_ge(s.p_inv, b + 1)
                    tt(P3, P3, per_head(rinv[:, :], NH), ALU.mult).then_inc(s.p_norm, 1)
                if do.X:
                    dve.wait_ge(s.sx, b)
                    red(mxx[:, :], X3, AX.X, ALU.max).then_inc(s.sx_max, 1)
                    dve.wait_ge(s.sx_max, b)
                    tt(X3, X3, per_head(mxx[:, :], NX), ALU.subtract).then_inc(s.sx_shift, 1)
                if do.Q:
                    rotate(b + 1)
                if do.X:
                    dve.wait_ge(s.px_exp, b)
                    red(denx[:, :], X3, AX.X, ALU.add).then_inc(s.px_sum, 1)
                    dve.wait_ge(s.px_sum, b)
                    nc.vector.reciprocal(rx[:, :], denx[:, :]).then_inc(s.px_inv, 1)
                if do.C:
                    c = b - 2
                    dve.wait_ge(s.lg_ps, c + 1)
                    nc.vector.tensor_copy(lgs[:, :], wb[2][0:T, 0:NE]).then_inc(s.lg, 1)
                    wait_alone(dve, s.lg, c + 1)
                    nc.vector.max(v8[:, :], lgs[:, :]).then_inc(s.top8, 1)
                    dve.wait_ge(s.top8, c + 1)
                    ts(d4[:, :], v8[:, 0:TOPK], v8[:, 0:1], None, ALU.subtract).then_inc(s.topd, 1)
                    nc.vector.max_index(i8[:, :], v8[:, :], lgs[:, :]).then_inc(s.topi, 1)
                    dve.wait_ge(s.topi, 2 * c + 1)
                    nc.vector.tensor_copy(idxf[:, :], i8[:, 0:TOPK]).then_inc(s.topi, 1)
                    dve.wait_ge(s.topi, 2 * c + 2)
                    oh3, ow3, pk3 = (t[:, :].rearrange("t (k e) -> t k e", e=NE) for t in (oh, ohw, pick))
                    tt(oh3, eid[:, :].rearrange("t (k e) -> t k e", e=NE), per_head(idxf[:, :], TOPK, NE),
                       ALU.is_equal).then_inc(s.onehot, 1)
                    dve.wait_ge(s.onehot, c + 1)
                    dve.wait_ge(s.rank_ps, c)
                    with nc.allow_low_precision(reason="sums of zeros and one"):
                        red(chosen[:, :], oh[:, :].rearrange("t (k e) -> t e k", e=NE), AX.X, ALU.add)\
                            .then_inc(s.chosen, 1)
                    dve.wait_ge(s.top_exp, c + 1)
                    nc.vector.reciprocal(inv4[:, :], sum4[:, :]).then_inc(s.top_inv, 1)
                    dve.wait_ge(s.top_inv, c + 1)
                    ts(w4[:, :], e4[:, :], inv4[:, 0:1], None, ALU.mult).then_inc(s.top_w, 1)
                    dve.wait_ge(s.top_w, c + 1)
                    tt(ow3, oh3, per_head(w4[:, :], TOPK, NE), ALU.mult).then_inc(s.ohw, 1)
                    dve.wait_ge(s.ohw, c + 1)
                    red(h3x[:, HID:HXW], ohw[:, :].rearrange("t (k e) -> t e k", e=NE), AX.X, ALU.add).then_inc(s.wd, 1)
                if do.Q:
                    norms(b + 1)
                if do.X:
                    dve.wait_ge(s.px_inv, b)
                    dve.wait_ge(s.avx_ps, b)
                    dve.wait_ge(s.oxT_ps, b - 1)
                    tt(ox[:, :].rearrange("t (i j d) -> t i j d", i=4, j=4),
                       wb[1][0:T, :].rearrange("t (i j d) -> t i j d", i=4, j=4),
                       rx[:, :].rearrange("t (j i) -> t i j", i=4).unsqueeze(3).to_broadcast([T, 4, 4, DX]),
                       ALU.mult).then_inc(s.ox, 1)
                if do.A:
                    dve.wait_ge(s.x1_ps, b + 1)
                    tt(row(b), row(b), wb[0][0:T, :], ALU.add).then_inc(s.x1, 1)
                    wait_alone(dve, s.x1, b + 1)
                    ln_stats(1, b, s.ln2_stats, s.ln2_var)
                if do.Q:
                    scale_keys(b + 1)
                if do.C:
                    c = b - 2
                    dve.wait_ge(s.rank_ps, c + 1)
                    tt(rk[:, :], wb[1][0:T, 0:NE], run[:, :], ALU.add).then_inc(s.rank, 1)
                    dve.wait_ge(s.rank, 2 * c + 1)
                    tt(run[:, :], wb[1][0:T, NE:2 * NE], run[:, :], ALU.add).then_inc(s.rank_used, 1)
                    tt(pick[:, :].rearrange("t (k e) -> t k e", e=NE), oh[:, :].rearrange("t (k e) -> t k e", e=NE),
                       rk[:, :].unsqueeze(1).to_broadcast([T, TOPK, NE]), ALU.mult).then_inc(s.rank, 1)
                    dve.wait_ge(s.rank, 2 * c + 2)
                    dve.wait_ge(s.rank_used, c + 1)
                    dve.wait_ge(s.scat, 64 * c)
                    with nc.allow_low_precision(reason="whole numbers under 2^24"):
                        red(slot[:, :], pick[:, :].rearrange("t (k e) -> t k e", e=NE), AX.X, ALU.add)\
                            .then_inc(s.slots, 1)
                    nc.vector.tensor_copy(tok[:, :], tokall[:, bass.ds(c, 1)]).then_inc(s.slots, 1)
                if do.A:
                    dve.wait_ge(s.ln2_rstd, b + 1)
                    dve.wait_ge(s.h2T_ps, b)
                    ts(h2, row(b), mv[1][:, 0:1], rstd[1][:, 0:1], ALU.subtract, ALU.mult).then_inc(s.ln2_h, 1)
                if do.X:
                    c = b - 1
                    dve.wait_ge(s.x2_ps, c + 1)
                    tt(row(c), row(c), wb[3][0:T, :], ALU.add).then_inc(s.x2, 1)
                    wait_alone(dve, s.x2, c + 1)
                    nc.vector.bn_stats(st[2][:, :], row(c)).then_inc(s.ln3_stats, 1)
                    wait_alone(dve, s.ln3_stats, 2 * c + 1)
                    nc.vector.bn_aggr(mv[2][:, :], st[2][:, :]).then_inc(s.ln3_stats, 1)
                    dve.wait_ge(s.ln3_stats, 2 * c + 2)
                    ts(var[2][:, 0:1], mv[2][:, 1:2], 1e-5, None, ALU.add).then_inc(s.ln3_g, 1)
                    ts(var[2][:, 1:2], mv[2][:, 1:2], 1.0 + 1e-6, 1e-11, ALU.mult, ALU.add).then_inc(s.ln3_var, 1)

            wait_alone(dve, s.ld_x0, 16)
            ln_stats(0, 0, s.ln1_stats, s.ln1_var)
            ln1_apply(0)
            joined(range(1, 12, 2))
            rotate(0)
            joined(range(13, 16, 2))
            norms(0)
            scale_keys(0)
            pipeline(dve, step)

            tt(rk[0:1, :], run[0:1, :], runs[0:1, :], ALU.subtract).then_inc(s.cnt_f, 1)
            dve.wait_ge(s.cnt_f, 1)
            nc.vector.tensor_copy(cnt[:, :], rk[0:1, :]).then_inc(s.cnt, 1)
            with nc.allow_low_precision(reason="whole numbers under 2^24"):
                red(most[:, :], rk[0:1, :], AX.X, ALU.max).then_inc(s.cnt, 1)

            dve.wait_ge(s.ln3_base, NB)
            def shared_inner(g):
                for f in range(4):
                    dve.wait_ge(s.sh_silu, 4 * g + f + 1)
                    dve.wait_ge(s.sh_u, 4 * g + f + 1)
                    dve.wait_ge(s.sh_y_ps, 4 * g)
                    tt(shact[:, QW * f:QW * (f + 1)], shtmp[:, :], qb[2 + f % 2][:, 0:QW], ALU.mult).then_inc(s.sh_act, 1)

            def shared_rows(g):
                for t in range(4):
                    dve.wait_ge(s.sh_y_ps, 4 * g + t + 1)
                    dve.wait_ge((s.sh_st0, s.sh_st1)[t % 2], 32 * g + 16 * (t // 2))
                    tt(ytile[t % 2][:, :], resid[:, bass.ds(4 * HID * g + HID * t, HID)], wb[t][0:T, :], ALU.add)\
                        .then_inc(s.sh_y, 1)

            with dve.Fori(0, 3) as g:
                shared_inner(g)
                shared_rows(g)
            dve.wait_ge(s.ix_ld, 16 * FAST)
            nc.vector.tensor_copy(ixf, ixr).then_inc(s.ix_f, 1)
            shared_inner(3)
            dve.wait_ge(s.ix_T, 1)
            nc.vector.tensor_copy(idx[:, :], qb[0][:, 0:2 * NE]).then_inc(s.idx, 1)
            shared_rows(3)

            def weights_low(e, u, part):
                dve.wait_ge(m.wh, 2 * e + 1 + part)
                c = (slice(0, 2048), slice(2048, WX))[part]
                tt(wl[u % 2][:, c], slots_w[u % RING][:, c], wh[u % 2][:, c].bitcast(fp32), ALU.subtract).then_inc(m.wl, 1)

            def rows_low(e, u):
                dve.wait_ge(m.xT_ps, e + 1)
                for j in range(FAST):
                    nc.vector.tensor_copy(wcol[u % RING][:, j:j + 1], Xg[u % 2][j][:, bass.ds(HID + e, 1)]).then_inc(m.wcol, 1)
                dve.wait_ge(m.xh, e + 1)
                tt(xl[u % 2][:, :], QS[:, 0:1024], xh[u % 2][:, :].bitcast(fp32), ALU.subtract).then_inc(m.xT, 1)

            def expert(e, u):
                more = not isinstance(e, int) or e + 1 < NE
                if more:
                    rows_low(e + 1, u + 1)
                    weights_low(e + 1, u + 1, 0)
                for v in range(2):
                    dve.wait_ge(m.act_s, 2 * e + 1 + v)
                    dve.wait_ge(m.eal, e)
                    tt(ea[:, 256 * v:256 * (v + 1)], et[:, 256 * v:256 * (v + 1)],
                       QS[:, 1280 + 512 * v:1536 + 512 * v], ALU.mult).then_inc(m.act, 1)
                dve.wait_ge(m.eah, e + 1)
                tt(el[:, :], ea, eh[:, :].bitcast(fp32), ALU.subtract).then_inc(m.eal, 1)
                if more:
                    weights_low(e + 1, u + 1, 1)

            weights_low(0, 0, 0)
            weights_low(0, 0, 1)
            rows_low(0, 0)
            expert(0, 0)
            with dve.Fori(0, NE // RING - 1) as r:
                for u in range(1, RING + 1):
                    expert(r * RING + u, u)
            for e in range(NE - 3, NE):
                expert(e, e)

            done = dve.alloc_register("dve_late")
            dve.reg_mov(done, 0)
            dve.wait_ge(s.cnt, 2)
            longest = dve.value_load(most[0:1, 0:1], min_val=0, max_val=NTOK)
            with dve.If(longest > BLK * FAST):
                with dve.Fori(0, NE) as e:
                    c = dve.value_load(cnt[0:1, bass.ds(e, 1)], min_val=0, max_val=NTOK)
                    with dve.If(c > BLK * FAST):
                        with dve.Fori(FAST, NBLK) as j:
                            with dve.If(c > BLK * j):
                                n = dve.snap(done)
                                dve.wait_ge(o.xT_ps, n + 1)
                                nc.vector.tensor_copy(XT[0][:, 0:512], QS[:, 0:512]).then_inc(o.xT, 1)
                                dve.wait_ge(o.act_s, n + 1)
                                tt(ea[:, 0:256], et[:, 0:256], QS[:, 1280:1536], ALU.mult).then_inc(o.act, 1)
                                dve.reg_add(done, done, 1)
                                dve.nop(nofuse=True)
                        dve.nop(nofuse=True)
                dve.nop(nofuse=True)

        @block.gpsimd
        def _(pool):
            def power(dst, src):
                return nc.gpsimd.tensor_tensor(out=dst, in0=src, in1=phalf[:, 0:src.shape[1]], op=ALU.pow)

            def on_rows(ap):
                return bass.IndirectOffsetOnAxis(ap, 0)

            def ln1(c):
                pool.wait_ge(s.ln1_var, c + 1)
                power(rstd[0][:, 0:1], var[0][:, 0:1]).then_inc(s.ln1_rstd, 1)

            def qk(c):
                pool.wait_ge(s.qk_var, c + 1)
                pool.wait_ge(s.s_scaled, 4 * c)
                power(rall[:, :], qkv_var[:, :]).then_inc(s.qk_rstd, 1)

            def step(b):
                do = stages(b)
                if do.Q:
                    ln1(b + 1)
                    qk(b + 1)
                if do.A:
                    pool.wait_ge(s.ln2_var, b + 1)
                    power(rstd[1][:, 0:1], var[1][:, 0:1]).then_inc(s.ln2_rstd, 1)
                if do.X:
                    pool.wait_ge(s.ln3_g, b)
                    pool.wait_ge(s.ln3_var, b)
                    power(rstd[2][:, :], var[2][:, :]).then_inc(s.ln3_rstd, 1)
                if do.C:
                    wait_alone(pool, s.slots, 2 * (b - 1))
                    for k in range(TOPK):
                        nc.gpsimd.indirect_dma_start(table, on_rows(slot[:, k:k + 1]), tok[:, :], None)\
                            .then_inc(s.scat, 16)

            wait_alone(pool, s.wqk, 1)
            ln1(0)
            qk(0)
            pool.wait_ge(s.pad_st, 48)
            pipeline(pool, step)

            pool.wait_ge(s.scat, 64 * NB)
            for j in range(FAST):
                pool.dma_start(ixr[NE * j:NE * (j + 1), :],
                               table.rearrange("(e n) o -> e (n o)", e=NE)[:, BLK * j:BLK * (j + 1)]).then_inc(s.ix_ld, 16)
            def shared_rows(g):
                for t in range(4):
                    dst = out[bass.ds(4 * T * g + T * t, T), :]
                    pool.wait_ge(s.sh_y, 4 * g + t + 1)
                    pool.dma_start(dst, ytile[t % 2][:, :]).then_inc((s.sh_st0, s.sh_st1)[t % 2], 16)

            with pool.Fori(0, 3) as g:
                shared_rows(g)

            def places(e, to, copies):
                nc.gpsimd.tensor_copy(to[:, :], idx[:, :].rearrange("p (j e) -> p j e", j=FAST)[:, :, bass.ds(e, 1)]
                                      .rearrange("p j e -> p (j e)")).then_inc(m.ix, 1)
                wait_alone(pool, m.ix, copies)

            def gather(e, u):
                if not isinstance(e, int) or e >= 2:
                    pool.wait_ge(m.xT, e - 1)
                    pool.wait_ge(m.wcol, FAST * (e - 1))
                places(e, ixg[u % 2], e + 1 if isinstance(e, int) and e < AHEAD else 2 * e - AHEAD + 1)
                for j in range(FAST):
                    nc.gpsimd.indirect_dma_start(Xg[u % 2][j], None, hx, on_rows(ixg[u % 2][:, j:j + 1])).then_inc(s.gath[u % 2], 16)

            def scatter(e, u):
                if not isinstance(e, int) or e >= 1:
                    pool.wait_ge(m.scat_add, 32 * (e - 1 if u == 1 else e))
                places(e, ixs[u % 2], e + NE + 1 if isinstance(e, int) and e >= NE - AHEAD else 2 * e + AHEAD + 2)
                pool.wait_ge(m.y_w, e + 1)
                wait_alone(pool, m.scat_add, 32 * e)
                for j in range(FAST):
                    nc.gpsimd.indirect_dma_start(out, on_rows(ixs[u % 2][:, j:j + 1]), Y[u % 2][:, 512 * j:512 * (j + 1)], None,
                                                 compute_op=ALU.add).then_inc(m.scat_add, 16)

            pool.wait_ge(s.idx, 1)
            pool.wait_ge(s.hx_st, 16 * NB)
            gather(0, 0)
            gather(1, 1)
            shared_rows(3)
            pool.wait_ge(s.sh_st0, 8 * NB)
            pool.wait_ge(s.sh_st1, 8 * NB)
            gather(2, 2)
            gather(3, 3)
            scatter(0, 0)
            with pool.Fori(0, (NE - AHEAD - 1) // 2) as r:
                for u in range(1, 3):
                    gather(r * 2 + u + AHEAD, u + AHEAD)
                    scatter(r * 2 + u, u)
            for e in range(NE - AHEAD, NE):
                scatter(e, e)
            pool.wait_ge(m.scat_add, 32 * NE)

            done = pool.alloc_register("pool_late")
            pool.reg_mov(done, 0)
            pool.wait_ge(s.cnt, 2)
            longest = pool.value_load(most[0:1, 0:1], min_val=0, max_val=NTOK)
            with pool.If(longest > BLK * FAST):
                with pool.Fori(0, NE) as e:
                    c = pool.value_load(cnt[0:1, bass.ds(e, 1)], min_val=0, max_val=NTOK)
                    with pool.If(c > BLK * FAST):
                        with pool.Fori(FAST, NBLK) as j:
                            with pool.If(c > BLK * j):
                                n = pool.snap(done)
                                wait_alone(pool, o.idx, 16 * n + 16)
                                nc.gpsimd.indirect_dma_start(Xg[0][0], None, hx, on_rows(oidx)).then_inc(o.g, 16)
                                wait_alone(pool, o.y_w, n + 1)
                                nc.gpsimd.indirect_dma_start(out, on_rows(oidx), Y[0][:, 0:512], None,
                                                             compute_op=ALU.add).then_inc(o.add, 16)
                                pool.wait_ge(o.add, 16 * n + 16)
                                pool.reg_add(done, done, 1)
                                pool.nop(nofuse=True)
                        pool.nop(nofuse=True)
                pool.nop(nofuse=True)

def kernel(**inputs):
    import numpy as np
    import concourse.bacc as bacc
    from concourse.bass_utils import run_bass_kernel_spmd

    np_bf16 = mybir.dt.np(bf16)
    f = {k: np.asarray(v) for k, v in inputs.items()}
    L = "L0_attn_"
    rep = lambda v: np.ascontiguousarray(np.broadcast_to(v[None, :], (T, v.shape[0])))
    arrays = {
        "x": f["x"],
        "ctxT": f["ctx_512"].transpose(0, 2, 1),
        "wq_comp": f[L + "wq_comp"], "wq_up": f[L + "wq_up"],
        "wkv": np.concatenate([f[L + "wk"], f[L + "wv"]], axis=1),
        "qn": rep(f[L + "q_norm_w"]), "kn": rep(f[L + "k_norm_w"]), "sink": rep(f[L + "sink_logit"]),
        "w1T": f[L + "out_w1"].transpose(0, 2, 1), "out_w2": f[L + "out_w2"],
        "WqT": f["L0_xattn_Wq"].T, "WkvT": f["L0_xattn_Wkv_expand"].T, "WoutT": f["L0_xattn_Wout"].T,
        "normw": rep(f["L0_ffn_norm_w"]), "routerT": f["L0_ffn_router_w"].T,
        "w1": f["L0_ffn_w1"], "w2": f["L0_ffn_w2"], "sg": f["L0_ffn_sg"], "su": f["L0_ffn_su"], "sd": f["L0_ffn_sd"],
    }
    inv = np.float32(1.0) / np.float32(10000.0) ** (np.arange(0, RD, 2, dtype=np.float32) / np.float32(RD))
    ang = (np.arange(T, dtype=np.float32)[:, None] * inv[None, :]).astype(np.float64)
    cos, sin = np.cos(ang).astype(np.float32), np.sin(ang).astype(np.float32)
    t = np.arange(T)
    causal = np.where(t[None, :] <= t[:, None], 0.0, NEG).astype(np_bf16)
    arrays |= {
        "c_ident": np.eye(P, dtype=np.float32),
        "c_cos": np.concatenate([cos, cos], axis=1), "c_sin": np.concatenate([-sin, sin], axis=1),
        "c_eid": np.tile(np.arange(NE, dtype=np.float32), (T, TOPK)),
        "c_runs": np.tile(CAP * np.arange(NE, dtype=np.float32), (T, 1)),
        "c_tok": (t[:, None] + T * np.arange(NB)[None, :]).astype(np.int32),
        "c_identb": np.eye(T, dtype=np.float32).astype(np_bf16),
        "c_mask": np.tile(causal, (1, QH)),
        "c_tri": (t[:, None] < t[None, :]).astype(np_bf16),
        "c_ones": np.ones((T, T), dtype=np_bf16),
        "c_table": (NTOK + np.arange(NE * CAP) % PADS).astype(np.int32).reshape(-1, 1),
        "c_zero": np.zeros((PADS, HXW), dtype=np.float32),
    }
    nc = bacc.Bacc("TRN2", target_bir_lowering=False, num_devices=1)
    arrays = {f"in_{k}": np.ascontiguousarray(v) for k, v in arrays.items()}
    aps = {k[3:]: nc.dram_tensor(k, v.shape, mybir.dt.from_np(v.dtype), kind="ExternalInput").ap()
           for k, v in arrays.items()}
    out = nc.dram_tensor("out_rows", (ROWS, HID), fp32, kind="ExternalOutput").ap()
    build(nc, aps, out)
    r = run_bass_kernel_spmd(nc, [arrays], core_ids=[0])
    return r.results[0]["out_rows"][0:NTOK].reshape(NB, T, HID)
```
